# Optimizing a Trainium2 kernel written in Bass

```python
import numpy as np
import jax
import jax.numpy as jnp

def _softmax(x, axis=-1):
    return jax.nn.softmax(x, axis=axis)

def _gelu(x):
    return jax.nn.gelu(x, approximate=True)

def _silu(x):
    return jax.nn.silu(x)

def _sigmoid(x):
    return jax.nn.sigmoid(x)

def _layernorm(x, axis=-1, eps=1e-05):
    m = jnp.mean(x, axis=axis, keepdims=True)
    v = jnp.var(x, axis=axis, keepdims=True)
    return (x - m) / jnp.sqrt(v + eps)

def _scatter_add(tgt, idx, src, axis=0):
    return tgt.at[idx].add(src)

def _segment_sum(src, seg, n):
    return jax.ops.segment_sum(src, seg, n)
kernel_name = 'mk_adj_preln_d2_adj_r2_9cb8e8'

def setup_inputs(seed: int=0):
    np.random.seed(seed)
    _w = jnp.asarray

    def _rec_inputs():
        import jax
        import jax.numpy as jnp
        _gk = jax.random.key(seed)
        x = -0.006082 + 1.001 * jax.random.normal(jax.random.fold_in(_gk, 1), (8192, 64), jnp.float32)
        _a = jax.random.bernoulli(jax.random.fold_in(_gk, 2), 0.000976562, (8192, 8192))
        _a = jnp.logical_or(_a, jnp.swapaxes(_a, -1, -2))
        _a = jnp.logical_or(_a, jnp.eye(8192, dtype=bool))
        adj = _a.astype(jnp.int32)
        return (x, adj)
    x, adj = _rec_inputs()

    def _L0_gnn_setup():
        import jax, jax.numpy as jnp
        import numpy as np
        ALPHA = 0.2
        NEG_INF = -9000000000000000.0
        key = jax.random.key(seed)
        k1, k2, k3, k4 = jax.random.split(key, 4)
        N, F_IN, F_OUT = (512, 64, 64)
        h = jax.random.normal(k1, (N, F_IN), dtype=jnp.float32)
        adj = jax.random.randint(k2, (N, N), 0, 2, dtype=jnp.int32)
        lim_W = 1.414 * np.sqrt(6.0 / (F_IN + F_OUT))
        W = jax.random.uniform(k3, (F_IN, F_OUT), minval=-lim_W, maxval=lim_W, dtype=jnp.float32)
        lim_a = 1.414 * np.sqrt(6.0 / (2 * F_OUT + 1))
        a = jax.random.uniform(k4, (2 * F_OUT, 1), minval=-lim_a, maxval=lim_a, dtype=jnp.float32)
        return {'h': h, 'adj': adj, 'W': W, 'a': a}
    _L0_gnn_all = _L0_gnn_setup()
    _L0_gnn_in = {k: v for k, v in _L0_gnn_all.items() if k in ('W', 'a')}
    del _L0_gnn_all

    def _L1_gnn_setup():
        import jax, jax.numpy as jnp
        import numpy as np
        N = 4096
        F_IN = 64
        F_OUT = 64
        ALPHA = 0.2
        NEG_INF = -9000000000000000.0
        key = jax.random.key(seed)
        k1, k2, k3, k4 = jax.random.split(key, 4)
        h = jax.random.normal(k1, (N, F_IN), dtype=jnp.float32)
        adj = jax.random.randint(k2, (N, N), 0, 2, dtype=jnp.int32)
        W = jax.random.normal(k3, (F_OUT, F_IN), dtype=jnp.float32) * (1.0 / np.sqrt(F_IN))
        a = jax.random.normal(k4, (2 * F_OUT,), dtype=jnp.float32) * (1.0 / np.sqrt(2 * F_OUT))
        return {'h': h, 'adj': adj, 'W': W, 'a': a}
    _L1_gnn_all = _L1_gnn_setup()
    _L1_gnn_in = {k: v for k, v in _L1_gnn_all.items() if k in ('W', 'a')}
    del _L1_gnn_all
    return {'x': x, 'adj': adj, 'L0_gnn_W': _L0_gnn_in['W'], 'L0_gnn_a': _L0_gnn_in['a'], 'L1_gnn_W': _L1_gnn_in['W'], 'L1_gnn_a': _L1_gnn_in['a']}

def reference(x, adj, L0_gnn_W, L0_gnn_a, L1_gnn_W, L1_gnn_a):
    import jax
    import jax.numpy as jnp

    def _L0_gnn_ref(h, adj, W, a):
        import jax, jax.numpy as jnp
        import numpy as np
        ALPHA = 0.2
        NEG_INF = -9000000000000000.0
        F_OUT = W.shape[1]
        Wh = h @ W
        a1, a2 = (a[:F_OUT, 0], a[F_OUT:, 0])
        e = (Wh @ a1)[:, None] + (Wh @ a2)[None, :]
        e = jax.nn.leaky_relu(e, negative_slope=ALPHA)
        scores = jnp.where(adj > 0, e, jnp.float32(NEG_INF))
        attention = jax.nn.softmax(scores, axis=1)
        h_prime = attention @ Wh
        return jax.nn.elu(h_prime)

    def _L1_gnn_ref(h, adj, W, a):
        import jax, jax.numpy as jnp
        import numpy as np
        N = 4096
        F_IN = 64
        F_OUT = 64
        ALPHA = 0.2
        NEG_INF = -9000000000000000.0
        Wh = h @ W.T
        a1, a2 = (a[:F_OUT], a[F_OUT:])
        src = Wh @ a1
        dst = Wh @ a2
        e = jax.nn.leaky_relu(src[:, None] + dst[None, :], negative_slope=ALPHA)
        scores = jnp.where(adj > 0, e, NEG_INF)
        attention = jax.nn.softmax(scores, axis=1)
        h_prime = attention @ Wh
        return jax.nn.elu(h_prime)
    h = jnp.maximum(_layernorm(x, axis=-1), 0.0)
    x = x + _L0_gnn_ref(h, adj, L0_gnn_W, L0_gnn_a)
    h = jnp.maximum(_layernorm(x, axis=-1), 0.0)
    x = x + _L1_gnn_ref(h, adj, L1_gnn_W, L1_gnn_a)
    return x

_drawn_inputs = setup_inputs


def setup_inputs(seed=0):
    import zlib

    import numpy as np

    out = dict(_drawn_inputs(seed))
    spreads = {}
    factors = {}
    for name, (base, spread) in spreads.items():
        noise = np.random.default_rng([zlib.crc32(name.encode()), seed]).standard_normal(out[name].shape)
        drawn = base * np.exp(spread * noise) if base else spread * noise
        out[name] = jnp.asarray(drawn.astype(out[name].dtype))
    for name, factor in factors.items():
        out[name] = (out[name] * factor).astype(out[name].dtype)
    return out
```

```python
from contextlib import ExitStack

import concourse.bass as bass
from concourse import mybir

P = 128
ALU = mybir.AluOpType
ACT = mybir.ActivationFunctionType
AX = mybir.AxisListType
F32 = mybir.dt.float32
BF16 = mybir.dt.bfloat16
FP8 = mybir.dt.float8e4
U8 = mybir.dt.uint8
U32 = mybir.dt.uint32

GROUP = 512
BLOCKS = GROUP // P
SEG = 8
CHUNK = 8
HALF = 4
ON = 0x40
AHEAD = 3
SLOTS = 4
SUMS_AT = 2


def build(nc, x, adj, w0, a0, w1, a1, out):
    N, F = x.shape
    JB = N // P
    NG = N // GROUP
    PAIRS = JB // 2
    SEGS = PAIRS // SEG
    CH = JB // CHUNK
    E = F + 1
    GC = 3 * E
    assert F == 64 and NG % 8 == 0 and PAIRS % SEG == 0

    x1 = nc.dram_tensor("x_after_layer0", [N, F], F32, kind="Internal").ap()

    with ExitStack() as ctx:
        def sb(name, shape, dt, c=ctx):
            return c.enter_context(nc.sbuf_tensor(name, shape, dt))

        def sem(name, c=ctx):
            return c.enter_context(nc.semaphore(name))

        packed = sb("packed", [P, JB, (NG // 8) * GROUP], U8)
        srow = sb("srow", [P, N], F32)
        G_flat = sb("G", [P, JB * 2 * GC], BF16)
        ident = sb("ident", [P, P], F32)
        identb = sb("identb", [P, P], BF16)
        negd = sb("negd", [P, JB], F32)
        scol = sb("scol", [P, JB], F32)
        alpha = sb("alpha", [P, JB], F32)
        beta = sb("beta", [P, JB], F32)
        csum = sb("csum", [P, F], F32)
        shifts = sb("shifts", [P, 8], U32)

        constants(nc, ident, identb, shifts, packed)
        for layer, (src, w, a, dst) in enumerate(((x, w0, a0, x1), (x1, w1, a1, out))):
            prologue(nc, layer, src, w, a, srow, G_flat, ident, negd, scol, alpha, beta, csum)
            main(nc, layer, src, adj, dst, packed, srow, G_flat, identb, negd, alpha, beta, csum, shifts)


def constants(nc, ident, identb, shifts, packed):
    with ExitStack() as ctx:
        zeroed = ctx.enter_context(nc.semaphore("ident_zeroed"))
        made = ctx.enter_context(nc.semaphore("ident_made"))
        block = ctx.enter_context(nc.Block())

        @block.gpsimd
        def _(pool):
            nc.gpsimd.memset(ident[:], 0.0).then_inc(zeroed, 1)
            pool.wait_ge(zeroed, 1)
            nc.gpsimd.affine_select(out=ident[:], in_=ident[:], compare_op=ALU.not_equal, fill=1.0, base=0,
                                    pattern=[[-1, P]], channel_multiplier=1).then_inc(made, 1)
            for k in range(8):
                nc.gpsimd.memset(shifts[:, k:k + 1], k)

        @block.vector
        def _(dve):
            nc.vector.memset(packed[:].rearrange("p a b -> p (a b)").bitcast(U32), 0)
            dve.wait_ge(made, 1)
            nc.vector.tensor_copy(identb[:], ident[:])


def prologue(nc, layer, src, w, a, srow, G_flat, ident, negd, scol, alpha, beta, csum):
    N, F = src.shape
    JB = N // P
    CH = JB // CHUNK
    E = F + 1
    T = CHUNK * P
    src_t = src.rearrange("(n p) f -> p n f", p=P)
    G = G_flat[:].rearrange("p (n c t e) -> p n c t e", c=2, t=3, e=E)
    L = f"{layer}"
    with ExitStack() as ctx:
        def sb(name, shape, dt=F32):
            return ctx.enter_context(nc.sbuf_tensor(name + L, shape, dt))

        def ps(name, shape, dt=F32):
            return ctx.enter_context(nc.psum_tensor(name + L, shape, dt))

        def sem(name):
            return ctx.enter_context(nc.semaphore(name + L))

        wnat = sb("wnat", [F, F])
        wT = sb("wT", [F, F])
        acols = sb("acols", [F, 2])
        arep = sb("arep", [F, P])
        ones = sb("ones", [F, P])
        wext = sb("wext", [F, F + 2])
        wsrep = sb("wsrep", [F, P])
        wd2 = sb("wd2", [F, 2])
        half = sb("half", [P, 1])
        mhalf = sb("mhalf", [P, CHUNK])
        bound2 = sb("bound2", [P, 1])
        bound = sb("bound", [P, 1])
        nbound = sb("nbound", [P, 2])
        xc = sb("xc", [P, 2, CHUNK, F])
        xm = sb("xm", [P, CHUNK, F])
        sq = sb("sq", [P, CHUNK, F])
        hn = sb("hn", [P, CHUNK, F])
        hT = sb("hT", [F, T])
        stats = sb("stats", [P, 5, CHUNK])
        fcol = sb("fcol", [P, 2, CHUNK])
        gf = sb("gf", [P, CHUNK, E])
        gr = sb("gr", [P, CHUNK, E])
        hsum = sb("hsum", [F, CH])
        hs1 = sb("hs1", [F, 1])
        hsrep = sb("hsrep", [F, P])
        tcol = sb("tcol", [P, 3, JB])

        psW = ps("psW", [P, 512])
        psT = ps("psT", [F, T])
        psS = ps("psS", [P, T])
        psWh = ps("psWh", [P, 2, 512])

        w_in = sem("w_in")
        consts_set = sem("consts_set")
        w_turned = sem("w_turned")
        w_ready = sem("w_ready")
        wa_done = sem("wa_done")
        wext_ready = sem("wext_ready")
        norm2_done = sem("norm2_done")
        bound2_ready = sem("bound2_ready")
        bound_made = sem("bound_made")
        bound_ready = sem("bound_ready")
        x_in = [sem("x_in_a"), sem("x_in_b")]
        dve_step = sem("dve_step")
        centred = sem("centred")
        squared = sem("squared")
        var_ready = sem("var_ready")
        rstd_ready = sem("rstd_ready")
        hn_ready = sem("hn_ready")
        turned = sem("turned")
        hT_ready = sem("hT_ready")
        s_done = sem("s_done")
        s_copied = sem("s_copied")
        wh_done = sem("wh_done")
        f_ready = sem("f_ready")
        gf_ready = sem("gf_ready")
        hi_ready = sem("hi_ready")
        rest_ready = sem("rest_ready")
        mid_ready = sem("mid_ready")
        g_done = sem("g_done")
        hsum_ready = sem("hsum_ready")
        csum_done = sem("csum_done")
        exps_in = sem("exps_in")
        block = ctx.enter_context(nc.Block())

        @block.sync
        def _(sp):
            sp.dma_start(wnat[:], w).then_inc(w_in, 16)
            av = a.rearrange("(t f) o -> f (t o)", t=2) if len(a.shape) == 2 else a.rearrange("(t f) -> f t", t=2)
            with nc.allow_non_contiguous_dma("128 floats"):
                sp.dma_start(acols[:], av).then_inc(w_in, 16)
            for q in range(CH):
                if q >= 2:
                    sp.wait_ge(centred, q - 1)
                sp.dma_start(xc[:, q % 2], src_t[:, q * CHUNK:(q + 1) * CHUNK, :]).then_inc(x_in[q % 2], 16)

        @block.gpsimd
        def _(pool):
            nc.gpsimd.memset(mhalf[:], -0.5).then_inc(consts_set, 1)
            nc.gpsimd.memset(half[:], 0.5).then_inc(consts_set, 1)
            nc.gpsimd.memset(ones[:], 1.0).then_inc(consts_set, 1)
            pool.wait_ge(consts_set, 3)
            pool.wait_ge(bound2_ready, 1)
            nc.gpsimd.tensor_tensor(bound[:], bound2[:], half[:], ALU.pow).then_inc(bound_made, 1)
            for q in range(CH):
                pool.wait_ge(var_ready, q + 1)
                nc.gpsimd.tensor_tensor(stats[:, 4, :], stats[:, 3, :], mhalf[:], ALU.pow).then_inc(rstd_ready, 1)

        @block.scalar
        def _(act):
            act.wait_ge(bound_ready, 2)
            for q in range(CH):
                act.wait_ge(centred, q + 1)
                nc.scalar.activation(sq[:], xm[:], ACT.Square).then_inc(squared, 1)
                act.wait_ge(turned, q + 1)
                if q >= 1:
                    act.wait_ge(wh_done, q)
                nc.scalar.activation(hT[:], psT[:], ACT.Relu, accum_out=hsum[:, q:q + 1]).then_inc(hT_ready, 1)
                act.wait_ge(wh_done, q + 1)
                d = psWh[:, :, 0:4 * (F + 2)].rearrange("p b (n e) -> p b n e", e=F + 2)[:, :, :, F]
                if q >= 1:
                    act.wait_ge(gf_ready, 2 * q)
                nc.scalar.activation(fcol[:, 0, :].rearrange("p (b n) -> p b n", b=2), d, ACT.Exp,
                                     bias=nbound[:, 0:1]).then_inc(f_ready, 1)
                nc.scalar.activation(fcol[:, 1, :].rearrange("p (b n) -> p b n", b=2), d, ACT.Exp,
                                     bias=nbound[:, 1:2], scale=0.2).then_inc(f_ready, 1)
                act.wait_ge(s_done, q + 1)
                nc.scalar.copy(srow[:, q * T:(q + 1) * T], psS[:]).then_inc(s_copied, 1)
                for c in range(2):
                    n = 2 * q + c
                    gq = G[:, q * CHUNK:(q + 1) * CHUNK, c]
                    act.wait_ge(gf_ready, n + 1)
                    nc.scalar.copy(gq[:, :, 0, :], gf[:]).then_inc(hi_ready, 1)
                    act.wait_ge(rest_ready, n + 1)
                    nc.scalar.copy(gq[:, :, 1, :], gr[:]).then_inc(mid_ready, 1)
            act.wait_ge(exps_in, 2)
            nc.scalar.activation(alpha[:], tcol[:, 1, :], ACT.Exp)
            nc.scalar.activation(beta[:], tcol[:, 2, :], ACT.Exp)

        @block.tensor
        def _(pe):
            pe.wait_ge(w_in, 32)
            nc.tensor.transpose(psW[0:F, 0:F], wnat[:], ident[0:F, 0:F]).then_inc(w_turned, 1)
            pe.wait_ge(w_ready, 3)
            wlhs = wT if layer == 0 else wnat
            nc.tensor.matmul(psW[0:F, 128:130], wlhs[:], acols[:], start=True, stop=True)
            nc.tensor.matmul(psW[0:F, 256:384], wlhs[:], arep[:], start=True, stop=True).then_inc(wa_done, 1)
            pe.wait_ge(wext_ready, 4)
            pe.wait_ge(consts_set, 3)
            nc.tensor.matmul(psW[:, 384:386], ones[:], wd2[:], start=True, stop=True).then_inc(norm2_done, 1)
            for q in range(CH):
                pe.wait_ge(hn_ready, q + 1)
                if q >= 1:
                    pe.wait_ge(hT_ready, q)
                for n in range(CHUNK):
                    t = nc.tensor.transpose(psT[:, n * P:(n + 1) * P], hn[:, n, :], ident[:])
                t.then_inc(turned, 1)
                pe.wait_ge(hT_ready, q + 1)
                if q >= 1:
                    pe.wait_ge(gf_ready, 2 * q)
                    pe.wait_ge(f_ready, 2 * q)
                    pe.wait_ge(s_copied, q)
                for n in range(CHUNK):
                    o = n % 4 * (F + 2)
                    m = nc.tensor.matmul(psWh[:, n // 4, o:o + F + 2], hT[:, n * P:(n + 1) * P], wext[:],
                                         start=True, stop=True)
                m.then_inc(wh_done, 1)
                for n in range(T // 512):
                    m = nc.tensor.matmul(psS[:, n * 512:(n + 1) * 512], wsrep[:], hT[:, n * 512:(n + 1) * 512],
                                         start=True, stop=True)
                m.then_inc(s_done, 1)
            pe.wait_ge(hsum_ready, 1)
            nc.tensor.matmul(psW[:, 0:F], hsrep[:], wext[:, 0:F], start=True, stop=True).then_inc(csum_done, 1)

        @block.vector
        def _(dve):
            steps = [0]

            def then(ins):
                steps[0] += 1
                ins.then_inc(dve_step, 1)
                dve.wait_ge(dve_step, steps[0])

            dve.wait_ge(w_in, 32)
            nc.vector.tensor_copy(arep[:], acols[:, 0:1].broadcast_to([F, P])).then_inc(w_ready, 1)
            dve.wait_ge(w_turned, 1)
            nc.vector.tensor_copy(wT[:], psW[0:F, 0:F]).then_inc(w_ready, 1)
            nc.vector.tensor_copy(wext[:, 0:F], wnat[:] if layer == 0 else psW[0:F, 0:F]).then_inc(w_ready, 1)
            dve.wait_ge(wa_done, 1)
            nc.vector.tensor_copy(wext[:, F:F + 1], psW[0:F, 129:130]).then_inc(wext_ready, 1)
            nc.vector.tensor_copy(wext[:, F + 1:F + 2], psW[0:F, 128:129]).then_inc(wext_ready, 1)
            nc.vector.tensor_copy(wsrep[:], psW[0:F, 256:384]).then_inc(wext_ready, 1)
            dve.wait_ge(wext_ready, 3)
            nc.vector.tensor_tensor(wd2[:], wext[:, F:F + 1].broadcast_to([F, 2]),
                                    wext[:, F:F + 1].broadcast_to([F, 2]), ALU.mult).then_inc(wext_ready, 1)
            dve.wait_ge(norm2_done, 1)
            nc.vector.tensor_scalar(bound2[:], psW[:, 384:385], F * 1.001, None, ALU.mult).then_inc(bound2_ready, 1)
            dve.wait_ge(bound_made, 1)
            nc.vector.tensor_scalar(nbound[:, 0:1], bound[:], -1.0, None, ALU.mult).then_inc(bound_ready, 1)
            nc.vector.tensor_scalar(nbound[:, 1:2], bound[:], -0.2, None, ALU.mult).then_inc(bound_ready, 1)
            for q in range(CH):
                xq = xc[:, q % 2]
                dve.wait_ge(x_in[q % 2], 16 * (q // 2 + 1))
                then(nc.vector.tensor_reduce(stats[:, 0, :], xq, AX.X, ALU.add))
                then(nc.vector.tensor_scalar(stats[:, 1, :], stats[:, 0, :], -1.0 / F, None, ALU.mult))
                if q >= 1:
                    dve.wait_ge(squared, q)
                nc.vector.tensor_tensor(xm[:], xq, stats[:, 1, :].unsqueeze(2).broadcast_to([P, CHUNK, F]),
                                        ALU.add).then_inc(centred, 1)
                dve.wait_ge(squared, q + 1)
                then(nc.vector.tensor_reduce(stats[:, 2, :], sq[:], AX.X, ALU.add))
                nc.vector.tensor_scalar(stats[:, 3, :], stats[:, 2, :], 1.0 / F, 1e-5, ALU.mult,
                                        ALU.add).then_inc(var_ready, 1)
                dve.wait_ge(rstd_ready, q + 1)
                if q >= 1:
                    dve.wait_ge(turned, q)
                nc.vector.tensor_tensor(hn[:], xm[:], stats[:, 4, :].unsqueeze(2).broadcast_to([P, CHUNK, F]),
                                        ALU.mult).then_inc(hn_ready, 1)
                dve.wait_ge(wh_done, q + 1)
                dve.wait_ge(f_ready, 2 * q + 2)
                wh = psWh[:, :, 0:4 * (F + 2)].rearrange("p b (n e) -> p b n e", e=F + 2)
                cols = slice(q * CHUNK, (q + 1) * CHUNK)
                for c in range(2):
                    n = 2 * q + c
                    gq = G[:, cols, c]
                    if n >= 1:
                        dve.wait_ge(hi_ready, n)
                        dve.wait_ge(mid_ready, n)
                    for b in range(2):
                        nc.vector.tensor_tensor(
                            gf[:, 4 * b:4 * b + 4, 0:F], wh[:, b, :, 0:F],
                            fcol[:, c, 4 * b:4 * b + 4].unsqueeze(2).broadcast_to([P, 4, F]), ALU.mult)
                    if c == 0:
                        nc.vector.tensor_scalar(negd[:, cols].rearrange("p (b n) -> p b n", b=2), wh[:, :, :, F],
                                                -1.0, None, ALU.mult)
                        nc.vector.tensor_copy(scol[:, cols].rearrange("p (b n) -> p b n", b=2), wh[:, :, :, F + 1])
                    nc.vector.tensor_copy(gf[:, :, F:E], fcol[:, c, :].unsqueeze(2)).then_inc(gf_ready, 1)
                    dve.wait_ge(gf_ready, n + 1)
                    dve.wait_ge(hi_ready, n + 1)
                    nc.vector.tensor_tensor(gr[:], gf[:], gq[:, :, 0, :], ALU.subtract).then_inc(rest_ready, 1)
                    dve.wait_ge(mid_ready, n + 1)
                    nc.vector.tensor_tensor(gq[:, :, 2, :], gr[:], gq[:, :, 1, :], ALU.subtract).then_inc(g_done, 1)
            dve.wait_ge(g_done, 2 * CH)
            then(nc.vector.tensor_scalar(tcol[:, 0, :], scol[:], bound[:, 0:1], 0.8, ALU.add, ALU.mult))
            nc.vector.tensor_scalar(tcol[:, 1, :], tcol[:, 0, :], 0.0, None, ALU.min).then_inc(exps_in, 1)
            nc.vector.tensor_scalar(tcol[:, 2, :], tcol[:, 0, :], -1.0, 0.0, ALU.mult, ALU.min).then_inc(exps_in, 1)
            dve.wait_ge(hT_ready, CH)
            then(nc.vector.tensor_reduce(hs1[:], hsum[:], AX.X, ALU.add))
            nc.vector.tensor_copy(hsrep[:], hs1[:, 0:1].broadcast_to([F, P])).then_inc(hsum_ready, 1)
            dve.wait_ge(csum_done, 1)
            nc.vector.tensor_copy(csum[:], psW[:, 0:F])


def main(nc, layer, src, adj, dst, packed, srow, G_flat, identb, negd, alpha, beta, csum, shifts):
    N, F = src.shape
    JB = N // P
    NG = N // GROUP
    PAIRS = JB // 2
    SEGS = PAIRS // SEG
    E = F + 1
    GC = 3 * E
    W2 = 2 * GROUP
    CPS = SEG * 2 // CHUNK
    HPS = SEG * 2 // HALF
    PPC = CHUNK // 2
    PPH = HALF // 2
    assert CPS == 2 and HPS == SLOTS and SEG % SLOTS == 0
    L = f"{layer}"
    adj_t = adj.rearrange("(g b p) j -> g p b j", p=P, b=BLOCKS)
    src_t = src.rearrange("(g b p) f -> g p b f", p=P, b=BLOCKS)
    dst_t = dst.rearrange("(g b p) f -> g p b f", p=P, b=BLOCKS)
    with ExitStack() as ctx:
        def sb(name, shape, dt=F32):
            return ctx.enter_context(nc.sbuf_tensor(name + L, shape, dt))

        def sem(name):
            return ctx.enter_context(nc.semaphore(name + L))

        gbuf = sb("gbuf", [P, 2, CHUNK * 2 * GC], BF16)
        adjb = sb("adjb", [P, SLOTS, BLOCKS, HALF * P], BF16) if layer == 0 else None
        m = sb("m", [P, SLOTS, W2], U8)
        c1 = sb("c1", [P, 2, W2], U8)
        a1 = sb("a1", [P, SLOTS, W2], U8)
        a2 = sb("a2", [P, SLOTS, W2], U8)
        R = sb("R", [P, BLOCKS, 2, E])
        nd = sb("nd", [P, BLOCKS, E])
        num = sb("num", [P, BLOCKS, F])
        v = sb("v", [P, BLOCKS, F])
        neg = sb("neg", [P, BLOCKS, F])
        ex = sb("ex", [P, BLOCKS, F])
        xg = sb("xg", [P, BLOCKS, F])
        og = sb("og", [P, BLOCKS, F])
        small = sb("small", [P, 4, BLOCKS])
        acc = ctx.enter_context(nc.psum_tensor("acc" + L, [P, BLOCKS, 512], F32))
        tp = ctx.enter_context(nc.psum_tensor("tp" + L, [P, SLOTS, W2], BF16)) if layer == 0 else None

        adj_in = [sem(f"adj_in{i}_") for i in range(SLOTS)]
        turned = sem("turned_pairs")
        m_ready = sem("m_ready")
        c1_ready = sem("c1_ready")
        a1_ready = sem("a1_ready")
        a2_ready = sem("a2_ready")
        m_on = sem("m_on")
        g_in = [sem("g_in_a"), sem("g_in_b")]
        pairs_done = sem("pairs_done")
        sums_read = sem("sums_read")
        pool_step = sem("pool_step")
        v_ready = sem("v_ready")
        ex_ready = sem("ex_ready")
        ex_summed = sem("ex_summed")
        out_ready = sem("out_ready")
        xg_in = sem("xg_in")
        stored = sem("stored")
        small_set = sem("small_set")
        pe_passed = sem("pe_passed")
        pool_passed = sem("pool_passed")
        block = ctx.enter_context(nc.Block())

        def u32(t):
            return t.bitcast(U32)

        def pair(g, s, i):
            return g * PAIRS + s * SEG + i

        def wait_past(eng, semaphore, value, first):
            if not first or value > 0:
                eng.wait_ge(semaphore, value)

        def groups(eng, body):
            body(0, True, False)
            with eng.Fori(1, NG - 1) as g:
                body(g, False, False)
            body(NG - 1, False, True)

        def copy_G(eng, copy, g, s, c, first):
            wait_past(eng, pairs_done, pair(g, s, PPC * (c + 1) - 2 * PPC), first)
            if layer == 0:
                eng.sem_inc(pool_passed, 1)
            part = CHUNK * 2 * GC
            copy(gbuf[:, c], G_flat[:, bass.ds((s * CPS + c) * part, part)]).then_inc(g_in[c], 1)

        @block.gpsimd
        def _(pool):
            nc.gpsimd.memset(small[:, 3, :], -1.0).then_inc(small_set, 1)
            pool.wait_ge(small_set, 1)

            def passed():
                pool.sem_inc(pool_passed, 1)

            def epilogue(g):
                STEPS = 11
                k = [0]

                def then(ins):
                    k[0] += 1
                    ins.then_inc(pool_step, 1)
                    pool.wait_ge(pool_step, g * STEPS + k[0])
                    passed()

                cols = bass.ds(g * BLOCKS, BLOCKS)
                pool.wait_ge(sums_read, g + 1)
                then(nc.gpsimd.tensor_tensor(R[:, :, 0, :], R[:, :, 0, :],
                                             alpha[:, cols].unsqueeze(2).broadcast_to([P, BLOCKS, E]), ALU.mult))
                then(nc.gpsimd.tensor_tensor(R[:, :, 1, :], R[:, :, 1, :],
                                             beta[:, cols].unsqueeze(2).broadcast_to([P, BLOCKS, E]), ALU.mult))
                then(nc.gpsimd.tensor_tensor(nd[:], R[:, :, 0, :], R[:, :, 1, :], ALU.add))
                then(nc.gpsimd.tensor_scalar(small[:, 0, :], nd[:, :, F], 0.0, None, ALU.is_equal))
                then(nc.gpsimd.tensor_scalar(small[:, 1, :], small[:, 0, :], float(N), None, ALU.mult))
                then(nc.gpsimd.tensor_tensor(small[:, 1, :], small[:, 1, :], nd[:, :, F], ALU.add))
                then(nc.gpsimd.tensor_tensor(small[:, 2, :], small[:, 1, :], small[:, 3, :], ALU.pow))
                then(nc.gpsimd.tensor_tensor(num[:], small[:, 0, :].unsqueeze(2).broadcast_to([P, BLOCKS, F]),
                                             csum[:].unsqueeze(1).broadcast_to([P, BLOCKS, F]), ALU.mult))
                then(nc.gpsimd.tensor_tensor(num[:], num[:], nd[:, :, 0:F], ALU.add))
                then(nc.gpsimd.tensor_tensor(v[:], num[:], small[:, 2, :].unsqueeze(2).broadcast_to([P, BLOCKS, F]),
                                             ALU.mult))
                nc.gpsimd.tensor_scalar(neg[:], v[:], 0.0, None, ALU.min).then_inc(v_ready, 1)
                then(nc.gpsimd.tensor_scalar(v[:], v[:], 0.0, -1.0, ALU.max, ALU.add))
                assert k[0] == STEPS

            def finish(g):
                pool.wait_ge(ex_ready, g + 1)
                nc.gpsimd.tensor_tensor(ex[:], ex[:], v[:], ALU.add).then_inc(ex_summed, 1)
                pool.wait_ge(ex_summed, g + 1)
                pool.wait_ge(xg_in, 16 * (g + 1))
                nc.gpsimd.tensor_tensor(og[:], ex[:], xg[:], ALU.add).then_inc(out_ready, 1)

            def segment(g, s, first):
                for c in range(CPS):
                    if layer == 0:
                        for h in (2 * c, 2 * c + 1):
                            wait_past(pool, turned, pair(g, s, PPH * (h + 1) - SLOTS * PPH), first)
                            pool.dma_start(adjb[:, h],
                                           adj_t[g, :, :, bass.ds((s * HPS + h) * (HALF * P), HALF * P)]
                                           ).then_inc(adj_in[h], 16)
                        copy_G(pool, lambda o, i: nc.gpsimd.tensor_copy(u32(o), u32(i)), g, s, c, first)
                    else:
                        for i in range(PPC * c, PPC * (c + 1)):
                            k = i % SLOTS
                            pool.wait_ge(a1_ready, pair(g, s, i + 1))
                            nc.gpsimd.tensor_tensor(u32(a2[:, k]), u32(m[:, k]), u32(a1[:, k]),
                                                    ALU.subtract).then_inc(a2_ready, 1)

            def body(g, first, last):
                segment(g, 0, first)
                if not first:
                    epilogue(g - 1)
                with pool.Fori(1, SEGS - 1) as s:
                    segment(g, s, False)
                if not first:
                    finish(g - 1)
                segment(g, SEGS - 1, False)
                if last:
                    epilogue(g)
                    finish(g)

            groups(pool, body)

        @block.sync
        def _(sp):
            sp.dma_start(xg[:], src_t[0]).then_inc(xg_in, 16)
            with sp.Fori(1, NG) as g:
                sp.wait_ge(out_ready, g)
                sp.dma_start(dst_t[g - 1], og[:]).then_inc(stored, 16)
                sp.wait_ge(stored, 16 * g)
                sp.dma_start(xg[:], src_t[g]).then_inc(xg_in, 16)
            sp.wait_ge(out_ready, NG)
            sp.dma_start(dst_t[NG - 1], og[:]).then_inc(stored, 16)
            sp.wait_ge(stored, 16 * NG)

        @block.scalar
        def _(act):
            def exp_of(g):
                act.wait_ge(v_ready, g + 1)
                nc.scalar.activation(ex[:], neg[:], ACT.Exp).then_inc(ex_ready, 1)

            def segment(g, s, first):
                if layer == 0:
                    for i in range(SEG):
                        k = i % SLOTS
                        act.wait_ge(turned, pair(g, s, i + 1))
                        wait_past(act, a2_ready, pair(g, s, i + 1 - SLOTS), first)
                        nc.scalar.activation(m[:, k], tp[:, k], ACT.Sign).then_inc(m_ready, 1)
                else:
                    for c in range(CPS):
                        copy_G(act, nc.scalar.copy, g, s, c, first)

            def body(g, first, last):
                segment(g, 0, first)
                segment(g, 1, False)
                if not first:
                    exp_of(g - 1)
                with act.Fori(2, SEGS) as s:
                    segment(g, s, False)
                if last:
                    exp_of(g)

            groups(act, body)

        @block.tensor
        def _(pe):
            def turn(g, s, i, first):
                if i >= SEG:
                    s, i, first = s + 1, i - SEG, False
                k = i % SLOTS
                if i % PPH == 0:
                    pe.wait_ge(adj_in[i // PPH], 16 * (g * SEGS + s + 1))
                wait_past(pe, m_ready, pair(g, s, i + 1 - SLOTS), first)
                for n in range(2):
                    for b in range(BLOCKS):
                        j = (2 * i + n) % HALF
                        t = nc.tensor.transpose(tp[:, k, n * GROUP + b * P:n * GROUP + (b + 1) * P],
                                                adjb[:, i // PPH, b, j * P:(j + 1) * P], identb[:])
                t.then_inc(turned, 1)

            def products(g, s, i, opening):
                k = i % SLOTS
                c = i // PPC
                if i % PPC == 0:
                    pe.wait_ge(g_in[c], g * SEGS + s + 1)
                pe.wait_ge(a1_ready, pair(g, s, i + 1))
                pe.wait_ge(a2_ready, pair(g, s, i + 1))
                pe.sem_inc(pe_passed, 1)
                for n in range(2):
                    for b in range(BLOCKS):
                        for which, tile in ((0, a1), (1, a2)):
                            q = nc.tensor.matmul(
                                acc[:, b, which * GC:(which + 1) * GC],
                                tile[:, k, n * GROUP + b * P:n * GROUP + (b + 1) * P].bitcast(FP8),
                                gbuf[:, c, ((2 * i + n) % CHUNK * 2 + which) * GC:((2 * i + n) % CHUNK * 2 + which + 1) * GC],
                                start=(opening and n == 0 and which == 0), stop=False, skip_group_check=True)
                q.then_inc(pairs_done, 1)

            def segment(g, s, first, opening, ending):
                for i in range(SEG):
                    if layer == 0 and not (ending and i + AHEAD >= SEG):
                        turn(g, s, i + AHEAD, first)
                    products(g, s, i, opening and i == 0)

            def body(g, first, last):
                if first and layer == 0:
                    for i in range(AHEAD):
                        turn(g, 0, i, True)
                if not first:
                    pe.wait_ge(sums_read, g)
                segment(g, 0, first, True, False)
                with pe.Fori(1, SEGS - 1 if last else SEGS) as s:
                    segment(g, s, False, False, False)
                if last:
                    segment(g, SEGS - 1, False, False, True)

            groups(pe, body)

        @block.vector
        def _(dve):
            def sums(g):
                dve.wait_ge(pairs_done, (g + 1) * PAIRS)
                if not isinstance(g, int) or g > 0:
                    dve.wait_ge(out_ready, g)
                for b in range(BLOCKS):
                    r = nc.vector.tensor_reduce(
                        R[:, b], acc[:, b, 0:2 * GC].rearrange("p (c t e) -> p c e t", c=2, t=3), AX.X, ALU.add)
                r.then_inc(sums_read, 1)

            def one_pair(g, s, i, first):
                k = i % SLOTS
                wait_past(dve, pairs_done, pair(g, s, i + 1 - SLOTS), first)
                for n in range(2):
                    jb = s * (2 * SEG) + 2 * i + n
                    cmp = nc.vector.tensor_scalar(
                        c1[:, i % 2, n * GROUP:(n + 1) * GROUP], srow[:, bass.ds(g * GROUP, GROUP)],
                        negd[:, bass.ds(jb, 1)], float(ON), ALU.is_gt, ALU.mult)
                cmp.then_inc(c1_ready, 1)
                bits = packed[:, bass.ds(s * (2 * SEG) + 2 * i, 2), bass.ds(g // 8 * GROUP, GROUP)].bitcast(U32)
                shift = shifts[:, bass.ds(g % 8, 1)]

                def wide(t):
                    return u32(t).rearrange("p (n i) -> p n i", n=2)
                if layer == 0:
                    dve.wait_ge(m_ready, pair(g, s, i + 1))
                    nc.vector.scalar_tensor_tensor(bits, wide(m[:, k]), shift, bits,
                                                   ALU.logical_shift_left, ALU.bitwise_or)
                    dve.wait_ge(c1_ready, pair(g, s, i + 1))
                    nc.vector.scalar_tensor_tensor(u32(a1[:, k]), u32(m[:, k]), 6, u32(c1[:, i % 2]),
                                                   ALU.logical_shift_left, ALU.bitwise_and).then_inc(a1_ready, 1)
                    dve.wait_ge(a1_ready, pair(g, s, i + 1))
                    nc.vector.scalar_tensor_tensor(u32(a2[:, k]), u32(m[:, k]), 6, u32(a1[:, k]),
                                                   ALU.logical_shift_left, ALU.bitwise_xor).then_inc(a2_ready, 1)
                else:
                    nc.vector.tensor_scalar(wide(m[:, k]), bits, shift, 0x01010101,
                                            ALU.logical_shift_right, ALU.bitwise_and).then_inc(m_ready, 1)
                    dve.wait_ge(m_ready, pair(g, s, i + 1))
                    nc.vector.tensor_scalar(u32(m[:, k]), u32(m[:, k]), 6, None,
                                            ALU.logical_shift_left).then_inc(m_on, 1)
                    dve.wait_ge(m_on, pair(g, s, i + 1))
                    nc.vector.tensor_tensor(u32(a1[:, k]), u32(m[:, k]), u32(c1[:, i % 2]),
                                            ALU.bitwise_and).then_inc(a1_ready, 1)

            def body(g, first, last):
                for i in range(SEG):
                    if i == SUMS_AT and not first:
                        sums(g - 1)
                    one_pair(g, 0, i, first)
                with dve.Fori(1, SEGS) as s:
                    for i in range(SEG):
                        one_pair(g, s, i, False)
                if last:
                    sums(g)

            groups(dve, body)


_INS = ["x", "adj", "L0_gnn_W", "L0_gnn_a", "L1_gnn_W", "L1_gnn_a"]


def kernel(**inputs):
    import numpy as _np
    import concourse.bacc as _bacc
    from concourse import mybir as _mybir
    from concourse.bass_utils import run_bass_kernel_spmd as _run

    nc = _bacc.Bacc("TRN2", target_bir_lowering=False, num_devices=1)
    arrays, args = {}, []
    for name in _INS:
        arr = _np.ascontiguousarray(inputs[name])
        arrays[f"in_{name}_dram"] = arr
        args.append(nc.dram_tensor(f"in_{name}_dram", arr.shape, _mybir.dt.from_np(arr.dtype),
                                   kind="ExternalInput").ap())
    out = nc.dram_tensor("out_0_dram", inputs["x"].shape, _mybir.dt.float32, kind="ExternalOutput").ap()
    build(nc, *args, out)
    r = _run(nc, [arrays], core_ids=[0])
    return r.results[0]["out_0_dram"]
```

```python
from contextlib import ExitStack

import concourse.bass as bass
from concourse import mybir

P = 128
ALU = mybir.AluOpType
ACT = mybir.ActivationFunctionType
AX = mybir.AxisListType
F32 = mybir.dt.float32
BF16 = mybir.dt.bfloat16
FP8 = mybir.dt.float8e4
U8 = mybir.dt.uint8
U32 = mybir.dt.uint32

GROUP = 512
BLOCKS = GROUP // P
SEG = 8
CHUNK = 8
HALF = 4
ON = 0x40
BIG = 1e30
AHEAD = 3
SLOTS = 4
SUMS_AT = 2


LOW = 7


def bit_of(g):
    return g % LOW if g < 2 * LOW else 7


def byte_of(g):
    return g - 2 * LOW if isinstance(g, int) and g >= 2 * LOW else g // LOW


def build(nc, x, adj, w0, a0, w1, a1, out):
    N, F = x.shape
    JB = N // P
    NG = N // GROUP
    PAIRS = JB // 2
    SEGS = PAIRS // SEG
    CH = JB // CHUNK
    E = F + 1
    GC = 3 * E
    assert F == 64 and NG % 8 == 0 and PAIRS % SEG == 0

    x1 = nc.dram_tensor("x_after_layer0", [N, F], F32, kind="Internal").ap()

    with ExitStack() as ctx:
        def sb(name, shape, dt, c=ctx):
            return c.enter_context(nc.sbuf_tensor(name, shape, dt))

        def sem(name, c=ctx):
            return c.enter_context(nc.semaphore(name))

        packed = sb("packed", [P, JB, (NG // 8) * GROUP], U8)
        srow = sb("srow", [P, N], F32)
        G_flat = sb("G", [P, JB * 2 * GC], BF16)
        ident = sb("ident", [P, P], F32)
        identb = sb("identb", [P, P], BF16)
        negd = sb("negd", [P, JB], F32)
        scol = sb("scol", [P, JB], F32)
        alpha = sb("alpha", [P, JB], F32)
        beta = sb("beta", [P, JB], F32)
        csum = sb("csum", [P, F], F32)
        bigd = sb("bigd", [P, JB], F32)
        to_bit = sb("to_bit", [P, NG], U32)
        to_on = sb("to_on", [P, NG], U32)

        constants(nc, ident, identb, to_bit, to_on, packed)
        for layer, (src, w, a, dst) in enumerate(((x, w0, a0, x1), (x1, w1, a1, out))):
            prologue(nc, layer, src, w, a, srow, G_flat, ident, negd, bigd, scol, alpha, beta, csum)
            main(nc, layer, src, adj, dst, packed, srow, G_flat, identb, negd, bigd, alpha, beta, csum, to_bit, to_on)


def constants(nc, ident, identb, to_bit, to_on, packed):
    with ExitStack() as ctx:
        zeroed = ctx.enter_context(nc.semaphore("ident_zeroed"))
        made = ctx.enter_context(nc.semaphore("ident_made"))
        block = ctx.enter_context(nc.Block())

        @block.gpsimd
        def _(pool):
            nc.gpsimd.memset(ident[:], 0.0).then_inc(zeroed, 1)
            pool.wait_ge(zeroed, 1)
            nc.gpsimd.affine_select(out=ident[:], in_=ident[:], compare_op=ALU.not_equal, fill=1.0, base=0,
                                    pattern=[[-1, P]], channel_multiplier=1).then_inc(made, 1)
            for g in range(to_bit.shape[1]):
                nc.gpsimd.memset(to_bit[:, g:g + 1], bit_of(g))
                nc.gpsimd.memset(to_on[:, g:g + 1], max(6 - bit_of(g), 0))

        @block.vector
        def _(dve):
            nc.vector.memset(packed[:].rearrange("p a b -> p (a b)").bitcast(U32), 0)
            dve.wait_ge(made, 1)
            nc.vector.tensor_copy(identb[:], ident[:])


def prologue(nc, layer, src, w, a, srow, G_flat, ident, negd, bigd, scol, alpha, beta, csum):
    N, F = src.shape
    JB = N // P
    CH = JB // CHUNK
    E = F + 1
    T = CHUNK * P
    src_t = src.rearrange("(n p) f -> p n f", p=P)
    G = G_flat[:].rearrange("p (n c t e) -> p n c t e", c=2, t=3, e=E)
    L = f"{layer}"
    with ExitStack() as ctx:
        def sb(name, shape, dt=F32):
            return ctx.enter_context(nc.sbuf_tensor(name + L, shape, dt))

        def ps(name, shape, dt=F32):
            return ctx.enter_context(nc.psum_tensor(name + L, shape, dt))

        def sem(name):
            return ctx.enter_context(nc.semaphore(name + L))

        F2 = 2 * F
        wstack = sb("wstack", [F2, F])
        wside = sb("wside", [F, F2])
        acols = sb("acols", [F, 2])
        ones = sb("ones", [P, P])
        wblk = sb("wblk", [F2, 2 * (F + 2)])
        wd2 = sb("wd2", [F2, 2])
        half = sb("half", [P, 1])
        mhalf = sb("mhalf", [P, CHUNK])
        bound2 = sb("bound2", [P, 1])
        bound = sb("bound", [P, 1])
        nbound = sb("nbound", [P, 2])
        xc = sb("xc", [P, 2, CHUNK, F])
        xm = sb("xm", [P, CHUNK, F])
        sq = sb("sq", [P, CHUNK, F])
        hn = sb("hn", [P, CHUNK, F])
        hT = sb("hT", [F2, T // 2])
        stats = sb("stats", [P, 5, CHUNK])
        fcol = sb("fcol", [P, 2, CHUNK])
        gf = sb("gf", [P, 2, CHUNK * E])
        gr = sb("gr", [P, 2, CHUNK * E])
        hsum = sb("hsum", [F2, CH])
        hs1 = sb("hs1", [F2, 1])
        hsrep = sb("hsrep", [F2, P])
        tcol = sb("tcol", [P, 3, JB])

        psW = ps("psW", [P, 512])
        psT = ps("psT", [F2, T // 2])
        psS = ps("psS", [P, T])
        psWh = ps("psWh", [P, 2, 512])

        w_in = sem("w_in")
        consts_set = sem("consts_set")
        blk_zeroed = sem("blk_zeroed")
        w_turned = sem("w_turned")
        w_ready = sem("w_ready")
        wa_done = sem("wa_done")
        wblk_ready = sem("wblk_ready")
        norm2_done = sem("norm2_done")
        bound2_ready = sem("bound2_ready")
        bound_made = sem("bound_made")
        bound_ready = sem("bound_ready")
        x_in = [sem("x_in_a"), sem("x_in_b")]
        dve_step = sem("dve_step")
        centred = sem("centred")
        squared = sem("squared")
        var_ready = sem("var_ready")
        rstd_ready = sem("rstd_ready")
        hn_ready = sem("hn_ready")
        turned = sem("turned")
        hT_ready = sem("hT_ready")
        s_ready = sem("s_ready")
        s_done = sem("s_done")
        s_copied = sem("s_copied")
        wh_done = sem("wh_done")
        f_ready = sem("f_ready")
        gf_ready = [sem("gf1_ready"), sem("gf2_ready")]
        hi_ready = [sem("hi1_ready"), sem("hi2_ready")]
        rest_ready = [sem("rest1_ready"), sem("rest2_ready")]
        mid_ready = [sem("mid1_ready"), sem("mid2_ready")]
        lo_ready = [sem("lo1_ready"), sem("lo2_ready")]
        hsum_ready = sem("hsum_ready")
        csum_done = sem("csum_done")
        exps_in = sem("exps_in")
        block = ctx.enter_context(nc.Block())

        def part_of(q, c, part):
            return G[:, q * CHUNK:(q + 1) * CHUNK, c, part, :]

        def blocks(t):
            return t.rearrange("p (n e) -> p n e", e=E)

        def rest(eng, q, c):
            eng.wait_ge(gf_ready[c], q + 1)
            eng.wait_ge(hi_ready[c], q + 1)
            if q >= 1:
                eng.wait_ge(mid_ready[c], q)
                eng.wait_ge(lo_ready[c], q)
            e = nc.vector if c == 0 else nc.gpsimd
            e.tensor_tensor(blocks(gr[:, c]), blocks(gf[:, c]), part_of(q, c, 0),
                            ALU.subtract).then_inc(rest_ready[c], 1)

        def low(eng, q, c):
            eng.wait_ge(rest_ready[c], q + 1)
            eng.wait_ge(mid_ready[c], q + 1)
            e = nc.vector if c == 0 else nc.gpsimd
            e.tensor_tensor(part_of(q, c, 2), blocks(gr[:, c]), part_of(q, c, 1),
                            ALU.subtract).then_inc(lo_ready[c], 1)

        @block.sync
        def _(sp):
            if layer == 0:
                sp.dma_start(wstack[0:F, :], w).then_inc(w_in, 16)
                sp.dma_start(wstack[F:F2, :], w).then_inc(w_in, 16)
            else:
                sp.dma_start(wside[:, 0:F], w).then_inc(w_in, 16)
                sp.dma_start(wside[:, F:F2], w).then_inc(w_in, 16)
            av = a.rearrange("(t f) o -> f (t o)", t=2) if len(a.shape) == 2 else a.rearrange("(t f) -> f t", t=2)
            with nc.allow_non_contiguous_dma("128 floats"):
                sp.dma_start(acols[:], av).then_inc(w_in, 16)
            for q in range(CH):
                if q >= 2:
                    sp.wait_ge(centred, q - 1)
                sp.dma_start(xc[:, q % 2], src_t[:, q * CHUNK:(q + 1) * CHUNK, :]).then_inc(x_in[q % 2], 16)

        @block.gpsimd
        def _(pool):
            nc.gpsimd.memset(wblk[:], 0.0).then_inc(blk_zeroed, 1)
            nc.gpsimd.memset(mhalf[:], -0.5).then_inc(consts_set, 1)
            nc.gpsimd.memset(half[:], 0.5).then_inc(consts_set, 1)
            nc.gpsimd.memset(ones[:], 1.0).then_inc(consts_set, 1)
            pool.wait_ge(consts_set, 3)
            pool.wait_ge(bound2_ready, 1)
            nc.gpsimd.tensor_tensor(bound[:], bound2[:], half[:], ALU.pow).then_inc(bound_made, 1)
            for q in range(CH + 1):
                if q < CH:
                    pool.wait_ge(var_ready, q + 1)
                    nc.gpsimd.tensor_tensor(stats[:, 4, :], stats[:, 3, :], mhalf[:], ALU.pow).then_inc(rstd_ready, 1)
                if q >= 1:
                    rest(pool, q - 1, 1)
                    low(pool, q - 1, 1)

        @block.scalar
        def _(act):
            def parts(q, c):
                act.wait_ge(gf_ready[c], q + 1)
                nc.scalar.copy(part_of(q, c, 0), blocks(gf[:, c])).then_inc(hi_ready[c], 1)

            def mids(q, c):
                act.wait_ge(rest_ready[c], q + 1)
                nc.scalar.copy(part_of(q, c, 1), blocks(gr[:, c])).then_inc(mid_ready[c], 1)

            act.wait_ge(bound_ready, 2)
            for q in range(CH + 1):
                if q < CH:
                    act.wait_ge(centred, q + 1)
                    nc.scalar.activation(sq[:], xm[:], ACT.Square).then_inc(squared, 1)
                if q >= 1:
                    parts(q - 1, 0)
                    parts(q - 1, 1)
                    mids(q - 1, 0)
                    mids(q - 1, 1)
                    act.wait_ge(s_done, q)
                    nc.scalar.copy(srow[:, (q - 1) * T:q * T], psS[:]).then_inc(s_copied, 1)
                if q < CH:
                    act.wait_ge(turned, q + 1)
                    nc.scalar.activation(hT[:], psT[:], ACT.Relu, accum_out=hsum[:, q:q + 1]).then_inc(hT_ready, 1)
                    act.wait_ge(wh_done, q + 1)
                    d = psWh[:, :, 0:4 * (F + 2)].rearrange("p b (n e) -> p b n e", e=F + 2)[:, :, :, F]
                    for c, scale in ((0, 1.0), (1, 0.2)):
                        if q >= 1:
                            act.wait_ge(gf_ready[c], q)
                        nc.scalar.activation(fcol[:, c, :].rearrange("p (b n) -> p b n", b=2), d, ACT.Exp,
                                             bias=nbound[:, c:c + 1], scale=scale).then_inc(f_ready, 1)
            act.wait_ge(exps_in, 2)
            nc.scalar.activation(alpha[:], tcol[:, 1, :], ACT.Exp)
            nc.scalar.activation(beta[:], tcol[:, 2, :], ACT.Exp)

        @block.tensor
        def _(pe):
            pe.wait_ge(w_in, 48)
            if layer == 0:
                nc.tensor.transpose(psW[0:F, 0:F2], wstack[:], ident[:]).then_inc(w_turned, 1)
            else:
                nc.tensor.transpose(psW[0:F2, 0:F], wside[:], ident[0:F, 0:F]).then_inc(w_turned, 1)
            pe.wait_ge(w_ready, 1)
            nc.tensor.matmul(psW[0:F2, 128:130], wside[:], acols[:], start=True, stop=True).then_inc(wa_done, 1)
            pe.wait_ge(wblk_ready, 7)
            pe.wait_ge(consts_set, 3)
            nc.tensor.matmul(psW[:, 384:386], ones[:], wd2[:], start=True, stop=True).then_inc(norm2_done, 1)
            for q in range(CH):
                pe.wait_ge(hn_ready, q + 1)
                if q >= 1:
                    pe.wait_ge(hT_ready, q)
                for n in range(CHUNK // 2):
                    t = nc.tensor.transpose(psT[:, n * P:(n + 1) * P],
                                            hn[:, 2 * n:2 * n + 2, :].rearrange("p n f -> p (n f)"), ident[:])
                t.then_inc(turned, 1)
                pe.wait_ge(hT_ready, q + 1)
                if q >= 1:
                    pe.wait_ge(f_ready, 2 * q)
                    pe.wait_ge(gf_ready[0], q)
                    pe.wait_ge(gf_ready[1], q)
                for n in range(CHUNK // 2):
                    o = n % 2 * 2 * (F + 2)
                    m = nc.tensor.matmul(psWh[:, n // 2, o:o + 2 * (F + 2)], hT[:, n * P:(n + 1) * P], wblk[:],
                                         start=True, stop=True)
                m.then_inc(wh_done, 1)
                pe.wait_ge(s_ready, q + 1)
                if q >= 1:
                    pe.wait_ge(s_copied, q)
                for n in range(CHUNK):
                    jb = q * CHUNK + n
                    m = nc.tensor.matmul(psS[:, n * P:(n + 1) * P], scol[:, jb:jb + 1].broadcast_to([P, P]), ident[:],
                                         start=True, stop=True)
                m.then_inc(s_done, 1)
            pe.wait_ge(hsum_ready, 1)
            pe.wait_ge(bound2_ready, 1)
            nc.tensor.matmul(psW[:, 0:F], hsrep[:], wstack[:], start=True, stop=True).then_inc(csum_done, 1)

        @block.vector
        def _(dve):
            steps = [0]

            def then(ins):
                steps[0] += 1
                ins.then_inc(dve_step, 1)
                dve.wait_ge(dve_step, steps[0])

            def centre(q):
                xq = xc[:, q % 2]
                dve.wait_ge(x_in[q % 2], 16 * (q // 2 + 1))
                then(nc.vector.tensor_reduce(stats[:, 0, :], xq, AX.X, ALU.add))
                then(nc.vector.tensor_scalar(stats[:, 1, :], stats[:, 0, :], -1.0 / F, None, ALU.mult))
                nc.vector.tensor_tensor(xm[:], xq, stats[:, 1, :].unsqueeze(2).broadcast_to([P, CHUNK, F]),
                                        ALU.add).then_inc(centred, 1)

            def variance(q):
                dve.wait_ge(squared, q + 1)
                then(nc.vector.tensor_reduce(stats[:, 2, :], sq[:], AX.X, ALU.add))
                nc.vector.tensor_scalar(stats[:, 3, :], stats[:, 2, :], 1.0 / F, 1e-5, ALU.mult,
                                        ALU.add).then_inc(var_ready, 1)

            def normed(q):
                dve.wait_ge(rstd_ready, q + 1)
                if q >= 1:
                    dve.wait_ge(turned, q)
                nc.vector.tensor_tensor(hn[:], xm[:], stats[:, 4, :].unsqueeze(2).broadcast_to([P, CHUNK, F]),
                                        ALU.mult).then_inc(hn_ready, 1)

            def factored(q, c):
                dve.wait_ge(wh_done, q + 1)
                dve.wait_ge(f_ready, 2 * q + 2)
                wh = psWh[:, :, 0:4 * (F + 2)].rearrange("p b (n e) -> p b n e", e=F + 2)
                cols = slice(q * CHUNK, (q + 1) * CHUNK)

                def two(t):
                    return t.rearrange("p (b n) -> p b n", b=2)
                if c == 0:
                    nc.vector.tensor_copy(two(scol[:, cols]), wh[:, :, :, F + 1]).then_inc(s_ready, 1)
                    nc.vector.tensor_scalar(two(negd[:, cols]), wh[:, :, :, F], -1.0, None, ALU.mult)
                    nc.vector.tensor_scalar(two(bigd[:, cols]), wh[:, :, :, F], BIG, None, ALU.mult)
                if q >= 1:
                    dve.wait_ge(hi_ready[c], q)
                    dve.wait_ge(rest_ready[c], q)
                for b in range(2):
                    nc.vector.tensor_tensor(
                        blocks(gf[:, c])[:, 4 * b:4 * b + 4, 0:F], wh[:, b, :, 0:F],
                        fcol[:, c, 4 * b:4 * b + 4].unsqueeze(2).broadcast_to([P, 4, F]), ALU.mult)
                nc.vector.tensor_copy(blocks(gf[:, c])[:, :, F:E], fcol[:, c, :].unsqueeze(2)).then_inc(gf_ready[c], 1)

            dve.wait_ge(w_in, 48)
            dve.wait_ge(blk_zeroed, 1)
            dve.wait_ge(w_turned, 1)
            if layer == 0:
                nc.vector.tensor_copy(wside[:], psW[0:F, 0:F2]).then_inc(w_ready, 1)
            else:
                nc.vector.tensor_copy(wstack[:], psW[0:F2, 0:F]).then_inc(w_ready, 1)
            dve.wait_ge(w_ready, 1)
            dve.wait_ge(wa_done, 1)
            for r in range(2):
                rows, o = slice(r * F, (r + 1) * F), r * (F + 2)
                nc.vector.tensor_copy(wblk[rows, o:o + F], wstack[rows, :]).then_inc(wblk_ready, 1)
                nc.vector.tensor_copy(wblk[rows, o + F:o + F + 1], psW[rows, 129:130]).then_inc(wblk_ready, 1)
                nc.vector.tensor_copy(wblk[rows, o + F + 1:o + F + 2], psW[rows, 128:129]).then_inc(wblk_ready, 1)
            then(nc.vector.tensor_copy(tcol[:, 0, 0:2], psW[:, 129:130].broadcast_to([P, 2])))
            nc.vector.tensor_tensor(wd2[:], tcol[:, 0, 0:2], tcol[:, 0, 0:2], ALU.mult).then_inc(wblk_ready, 1)
            centre(0)
            dve.wait_ge(norm2_done, 1)
            nc.vector.tensor_scalar(bound2[:], psW[:, 384:385], 0.5 * F * 1.001, None,
                                    ALU.mult).then_inc(bound2_ready, 1)
            dve.wait_ge(bound_made, 1)
            nc.vector.tensor_scalar(nbound[:, 0:1], bound[:], -1.0, None, ALU.mult).then_inc(bound_ready, 1)
            nc.vector.tensor_scalar(nbound[:, 1:2], bound[:], -0.2, None, ALU.mult).then_inc(bound_ready, 1)
            for q in range(CH + 1):
                if 1 <= q < CH:
                    centre(q)
                if q >= 1:
                    factored(q - 1, 0)
                if q < CH:
                    variance(q)
                if q >= 1:
                    factored(q - 1, 1)
                if q < CH:
                    normed(q)
                if q >= 1:
                    rest(dve, q - 1, 0)
                    low(dve, q - 1, 0)
            then(nc.vector.tensor_scalar(tcol[:, 0, :], scol[:], bound[:, 0:1], 0.8, ALU.add, ALU.mult))
            nc.vector.tensor_scalar(tcol[:, 1, :], tcol[:, 0, :], 0.0, None, ALU.min).then_inc(exps_in, 1)
            nc.vector.tensor_scalar(tcol[:, 2, :], tcol[:, 0, :], -1.0, 0.0, ALU.mult, ALU.min).then_inc(exps_in, 1)
            dve.wait_ge(hT_ready, CH)
            then(nc.vector.tensor_reduce(hs1[:], hsum[:], AX.X, ALU.add))
            nc.vector.tensor_copy(hsrep[:], hs1[:, 0:1].broadcast_to([F2, P])).then_inc(hsum_ready, 1)
            dve.wait_ge(csum_done, 1)
            nc.vector.tensor_copy(csum[:], psW[:, 0:F])


def main(nc, layer, src, adj, dst, packed, srow, G_flat, identb, negd, bigd, alpha, beta, csum, to_bit, to_on):
    N, F = src.shape
    JB = N // P
    NG = N // GROUP
    PAIRS = JB // 2
    SEGS = PAIRS // SEG
    E = F + 1
    GC = 3 * E
    W2 = 2 * GROUP
    CPS = SEG * 2 // CHUNK
    HPS = SEG * 2 // HALF
    PPC = CHUNK // 2
    PPH = HALF // 2
    assert CPS == 2 and HPS == SLOTS and SEG % SLOTS == 0
    L = f"{layer}"
    adj_t = adj.rearrange("(g b p) j -> g p b j", p=P, b=BLOCKS)
    src_t = src.rearrange("(g b p) f -> g p b f", p=P, b=BLOCKS)
    dst_t = dst.rearrange("(g b p) f -> g p b f", p=P, b=BLOCKS)
    with ExitStack() as ctx:
        def sb(name, shape, dt=F32):
            return ctx.enter_context(nc.sbuf_tensor(name + L, shape, dt))

        def sem(name):
            return ctx.enter_context(nc.semaphore(name + L))

        gbuf = sb("gbuf", [P, 2, CHUNK * 2 * GC], BF16)
        adjb = sb("adjb", [P, SLOTS, BLOCKS, HALF * P], BF16) if layer == 0 else None
        m01 = sb("m01", [P, SLOTS, W2], U8) if layer == 0 else None
        mon = sb("mon", [P, SLOTS, W2], U8)
        c1 = sb("c1", [P, 2, W2], U8)
        a1 = sb("a1", [P, SLOTS, W2], U8)
        a2 = sb("a2", [P, SLOTS, W2], U8)
        R = sb("R", [P, BLOCKS, 2, E])
        nd = sb("nd", [P, BLOCKS, E])
        v = sb("v", [P, BLOCKS, F])
        neg = sb("neg", [P, BLOCKS, F])
        ex = sb("ex", [P, BLOCKS, F])
        xg = sb("xg", [P, BLOCKS, F])
        small = sb("small", [P, 4, BLOCKS])
        acc = ctx.enter_context(nc.psum_tensor("acc" + L, [P, BLOCKS, 512], F32))
        tp = ctx.enter_context(nc.psum_tensor("tp" + L, [P, SLOTS, W2], BF16)) if layer == 0 else None

        adj_in = [sem(f"adj_in{i}_") for i in range(SLOTS)]
        turned = sem("turned_pairs")
        m01_ready = sem("m01_ready")
        m01_packed = sem("m01_packed")
        mon_ready = sem("mon_ready")
        c1_dve = sem("c1_dve")
        c1_act = sem("c1_act")
        a1_ready = sem("a1_ready")
        a2_ready = sem("a2_ready")
        g_in = [sem("g_in_a"), sem("g_in_b")]
        pairs_done = sem("pairs_done")
        sums_read = sem("sums_read")
        pool_step = sem("pool_step")
        v_ready = sem("v_ready")
        ex_ready = sem("ex_ready")
        out_ready = sem("out_ready")
        xg_in = sem("xg_in")
        stored = sem("stored")
        small_set = sem("small_set")
        pe_passed = sem("pe_passed")
        pool_passed = sem("pool_passed")
        act_passed = sem("act_passed")
        block = ctx.enter_context(nc.Block())

        def u32(t):
            return t.bitcast(U32)

        def pair(g, s, i):
            return g * PAIRS + s * SEG + i

        def wait_past(eng, semaphore, value, first):
            if not first or value > 0:
                eng.wait_ge(semaphore, value)

        def groups(eng, body):
            body(0, True, False)
            with eng.Fori(1, 2 * LOW) as g:
                body(g, False, False)
            for g in range(2 * LOW, NG):
                body(g, False, g == NG - 1)

        @block.gpsimd
        def _(pool):
            nc.gpsimd.memset(small[:, 3, :], -1.0).then_inc(small_set, 1)
            pool.wait_ge(small_set, 1)
            STEPS = 12

            def output_steps(g):
                def spread(t, n):
                    return t.unsqueeze(2).broadcast_to([P, BLOCKS, n])

                cols = bass.ds(g * BLOCKS, BLOCKS)
                tt, ts = nc.gpsimd.tensor_tensor, nc.gpsimd.tensor_scalar
                return [
                    lambda: tt(R[:, :, 0, :], R[:, :, 0, :], spread(alpha[:, cols], E), ALU.mult),
                    lambda: tt(R[:, :, 1, :], R[:, :, 1, :], spread(beta[:, cols], E), ALU.mult),
                    lambda: tt(nd[:], R[:, :, 0, :], R[:, :, 1, :], ALU.add),
                    lambda: ts(small[:, 0, :], nd[:, :, F], 0.0, None, ALU.is_equal),
                    lambda: ts(small[:, 1, :], small[:, 0, :], float(N), None, ALU.mult),
                    lambda: tt(small[:, 1, :], small[:, 1, :], nd[:, :, F], ALU.add),
                    lambda: tt(small[:, 2, :], small[:, 1, :], small[:, 3, :], ALU.pow),
                    lambda: tt(v[:], spread(small[:, 0, :], F), csum[:].unsqueeze(1).broadcast_to([P, BLOCKS, F]),
                               ALU.mult),
                    lambda: tt(v[:], v[:], nd[:, :, 0:F], ALU.add),
                    lambda: tt(v[:], v[:], spread(small[:, 2, :], F), ALU.mult),
                    lambda: ts(neg[:], v[:], 0.0, None, ALU.min),
                    lambda: ts(v[:], v[:], 0.0, -1.0, ALU.max, ALU.add),
                ]

            def output_step(g, k):
                if k == 0:
                    pool.wait_ge(sums_read, g + 1)
                elif k == STEPS:
                    pool.wait_ge(ex_ready, g + 1)
                    nc.gpsimd.tensor_tensor(ex[:], ex[:], v[:], ALU.add).then_inc(pool_step, 1)
                    return
                elif k == STEPS + 1:
                    pool.wait_ge(pool_step, g * (STEPS + 1) + k)
                    pool.wait_ge(xg_in, 16 * (g + 1))
                    nc.gpsimd.tensor_tensor(xg[:], ex[:], xg[:], ALU.add).then_inc(out_ready, 1)
                    return
                else:
                    pool.wait_ge(pool_step, g * (STEPS + 1) + k)
                pool.sem_inc(pool_passed, 1)
                output_steps(g)[k]().then_inc(pool_step, 1)
                if k == STEPS - 1:
                    pool.wait_ge(pool_step, g * (STEPS + 1) + STEPS)
                    pool.sem_inc(v_ready, 1)

            def load_adj(g, s, h):
                pool.dma_start(adjb[:, h], adj_t[g, :, :, bass.ds((s * HPS + h) * (HALF * P), HALF * P)]
                               ).then_inc(adj_in[h], 16)

            def segment(g, s, last, steps=()):
                for i in range(SEG):
                    k = i % SLOTS
                    pool.wait_ge(a1_ready, pair(g, s, i + 1))
                    nc.gpsimd.tensor_tensor(u32(a2[:, k]), u32(mon[:, k]), u32(a1[:, k]),
                                            ALU.subtract).then_inc(a2_ready, 1)
                    ending = isinstance(s, int) and s == SEGS - 1
                    if layer == 0 and i % PPH == 0 and not (last and ending):
                        pool.wait_ge(turned, pair(g, s, i + PPH))
                        load_adj(g + 1 if ending else g, 0 if ending else s + 1, i // PPH)
                    if i < len(steps):
                        output_step(g - 1, steps[i])

            def body(g, first, last):
                if first and layer == 0:
                    for h in range(HPS):
                        load_adj(0, 0, h)
                if first:
                    segment(g, 0, last)
                    with pool.Fori(1, SEGS - 1) as s:
                        segment(g, s, last)
                    segment(g, SEGS - 1, last)
                else:
                    segment(g, 0, last)
                    segment(g, 1, last, range(0, SEG))
                    segment(g, 2, last, range(SEG, STEPS))
                    segment(g, 3, last, (STEPS, STEPS + 1))
                if last:
                    for k in range(STEPS + 2):
                        output_step(g, k)

            assert SEGS == 4
            groups(pool, body)

        @block.sync
        def _(sp):
            def copy_G(g, s, c, first):
                wait_past(sp, pairs_done, pair(g, s, PPC * (c + 1) - 2 * PPC), first)
                part = CHUNK * 2 * GC
                sp.dma_start(gbuf[:, c], G_flat[:, bass.ds((s * CPS + c) * part, part)]).then_inc(g_in[c], 16)

            def store(g):
                sp.wait_ge(out_ready, g + 1)
                sp.dma_start(dst_t[g], xg[:]).then_inc(stored, 16)

            def body(g, first, last):
                for c in range(CPS):
                    copy_G(g, 0, c, first)
                with sp.Fori(1, SEGS) as s:
                    for c in range(CPS):
                        copy_G(g, s, c, False)
                if not first:
                    store(g - 1)
                    sp.wait_ge(stored, 16 * g)
                sp.dma_start(xg[:], src_t[g]).then_inc(xg_in, 16)
                if last:
                    store(g)
                    sp.wait_ge(stored, 16 * NG)

            groups(sp, body)

        @block.scalar
        def _(act):
            def segment(g, s, first):
                for i in range(SEG):
                    k = i % SLOTS
                    jb = s * (2 * SEG) + 2 * i + 1
                    wait_past(act, a1_ready, pair(g, s, i + 1 - 2), first)
                    if not first or i >= 2:
                        act.sem_inc(act_passed, 1)
                    nc.scalar.activation(c1[:, i % 2, GROUP:W2], srow[:, bass.ds(g * GROUP, GROUP)], ACT.Relu,
                                         bias=bigd[:, bass.ds(jb, 1)], scale=BIG).then_inc(c1_act, 1)
                    if layer == 0:
                        act.wait_ge(turned, pair(g, s, i + 1))
                        wait_past(act, m01_packed, pair(g, s, i + 1 - SLOTS), first)
                        nc.scalar.activation(m01[:, k], tp[:, k], ACT.Sign).then_inc(m01_ready, 1)

            def exp_of(g):
                act.wait_ge(v_ready, g + 1)
                nc.scalar.activation(ex[:], neg[:], ACT.Exp).then_inc(ex_ready, 1)

            def body(g, first, last):
                segment(g, 0, first)
                with act.Fori(1, SEGS - 1) as s:
                    segment(g, s, False)
                if not first:
                    exp_of(g - 1)
                segment(g, SEGS - 1, False)
                if last:
                    exp_of(g)

            groups(act, body)

        @block.tensor
        def _(pe):
            def turn(g, s, i, first):
                if i >= SEG:
                    s, i, first = s + 1, i - SEG, False
                k = i % SLOTS
                if i % PPH == 0:
                    pe.wait_ge(adj_in[i // PPH], 16 * (g * SEGS + s + 1))
                wait_past(pe, m01_ready, pair(g, s, i + 1 - SLOTS), first)
                for n in range(2):
                    for b in range(BLOCKS):
                        j = (2 * i + n) % HALF
                        t = nc.tensor.transpose(tp[:, k, n * GROUP + b * P:n * GROUP + (b + 1) * P],
                                                adjb[:, i // PPH, b, j * P:(j + 1) * P], identb[:])
                t.then_inc(turned, 1)

            def products(g, s, i, opening):
                k = i % SLOTS
                c = i // PPC
                if i % PPC == 0:
                    pe.wait_ge(g_in[c], 16 * (g * SEGS + s + 1))
                pe.wait_ge(a1_ready, pair(g, s, i + 1))
                pe.wait_ge(a2_ready, pair(g, s, i + 1))
                pe.sem_inc(pe_passed, 1)
                for n in range(2):
                    for b in range(BLOCKS):
                        for which, tile in ((0, a1), (1, a2)):
                            at = ((2 * i + n) % CHUNK * 2 + which) * GC
                            q = nc.tensor.matmul(
                                acc[:, b, which * GC:(which + 1) * GC],
                                tile[:, k, n * GROUP + b * P:n * GROUP + (b + 1) * P].bitcast(FP8),
                                gbuf[:, c, at:at + GC],
                                start=(opening and n == 0 and which == 0), stop=False, skip_group_check=True)
                q.then_inc(pairs_done, 1)

            def segment(g, s, first, opening, ending):
                for i in range(SEG):
                    if layer == 0 and not (ending and i + AHEAD >= SEG):
                        turn(g, s, i + AHEAD, first)
                    products(g, s, i, opening and i == 0)

            def body(g, first, last):
                if first and layer == 0:
                    for i in range(AHEAD):
                        turn(g, 0, i, True)
                if not first:
                    pe.wait_ge(sums_read, g)
                segment(g, 0, first, True, False)
                with pe.Fori(1, SEGS - 1 if last else SEGS) as s:
                    segment(g, s, False, False, False)
                if last:
                    segment(g, SEGS - 1, False, False, True)

            groups(pe, body)

        @block.vector
        def _(dve):
            def sums(g):
                dve.wait_ge(pairs_done, (g + 1) * PAIRS)
                if not isinstance(g, int) or g > 0:
                    dve.wait_ge(out_ready, g)
                for b in range(BLOCKS):
                    r = nc.vector.tensor_reduce(
                        R[:, b], acc[:, b, 0:2 * GC].rearrange("p (c t e) -> p c e t", c=2, t=3), AX.X, ALU.add)
                r.then_inc(sums_read, 1)

            def one_pair(g, s, i, first):
                k = i % SLOTS
                wait_past(dve, pairs_done, pair(g, s, i + 1 - SLOTS), first)
                bits = packed[:, bass.ds(s * (2 * SEG) + 2 * i, 2), bass.ds(byte_of(g) * GROUP, GROUP)].bitcast(U32)

                def wide(t):
                    return u32(t).rearrange("p (n i) -> p n i", n=2)

                if layer == 0:
                    dve.wait_ge(m01_ready, pair(g, s, i + 1))
                    nc.vector.tensor_scalar(u32(mon[:, k]), u32(m01[:, k]), 6, None,
                                            ALU.logical_shift_left).then_inc(mon_ready, 1)
                elif isinstance(g, int) and g >= 2 * LOW:
                    nc.vector.tensor_scalar(wide(mon[:, k]), bits, 1, ON * 0x01010101,
                                            ALU.logical_shift_right, ALU.bitwise_and).then_inc(mon_ready, 1)
                else:
                    nc.vector.tensor_scalar(wide(mon[:, k]), bits, to_on[:, bass.ds(g, 1)], ON * 0x01010101,
                                            ALU.logical_shift_left, ALU.bitwise_and).then_inc(mon_ready, 1)
                nc.vector.tensor_scalar(c1[:, i % 2, 0:GROUP], srow[:, bass.ds(g * GROUP, GROUP)],
                                        negd[:, bass.ds(s * (2 * SEG) + 2 * i, 1)], float(ON),
                                        ALU.is_gt, ALU.mult).then_inc(c1_dve, 1)
                if layer == 0:
                    nc.vector.scalar_tensor_tensor(bits, wide(m01[:, k]), to_bit[:, bass.ds(g, 1)], bits,
                                                   ALU.logical_shift_left, ALU.bitwise_or).then_inc(m01_packed, 1)
                dve.wait_ge(mon_ready, pair(g, s, i + 1))
                dve.wait_ge(c1_act, pair(g, s, i + 1))
                dve.wait_ge(c1_dve, pair(g, s, i + 1))
                nc.vector.tensor_tensor(u32(a1[:, k]), u32(mon[:, k]), u32(c1[:, i % 2]),
                                        ALU.bitwise_and).then_inc(a1_ready, 1)

            def body(g, first, last):
                for i in range(SEG):
                    if i == SUMS_AT and not first:
                        sums(g - 1)
                    one_pair(g, 0, i, first)
                with dve.Fori(1, SEGS) as s:
                    for i in range(SEG):
                        one_pair(g, s, i, False)
                if last:
                    sums(g)

            groups(dve, body)


_INS = ["x", "adj", "L0_gnn_W", "L0_gnn_a", "L1_gnn_W", "L1_gnn_a"]


def kernel(**inputs):
    import numpy as _np
    import concourse.bacc as _bacc
    from concourse import mybir as _mybir
    from concourse.bass_utils import run_bass_kernel_spmd as _run

    nc = _bacc.Bacc("TRN2", target_bir_lowering=False, num_devices=1)
    arrays, args = {}, []
    for name in _INS:
        arr = _np.ascontiguousarray(inputs[name])
        arrays[f"in_{name}_dram"] = arr
        args.append(nc.dram_tensor(f"in_{name}_dram", arr.shape, _mybir.dt.from_np(arr.dtype),
                                   kind="ExternalInput").ap())
    out = nc.dram_tensor("out_0_dram", inputs["x"].shape, _mybir.dt.float32, kind="ExternalOutput").ap()
    build(nc, *args, out)
    r = _run(nc, [arrays], core_ids=[0])
    return r.results[0]["out_0_dram"]
```

```python
from contextlib import ExitStack

import concourse.bass as bass
from concourse import mybir

P = 128
ALU = mybir.AluOpType
ACT = mybir.ActivationFunctionType
AX = mybir.AxisListType
F32 = mybir.dt.float32
BF16 = mybir.dt.bfloat16
F16 = mybir.dt.float16
FP8 = mybir.dt.float8e4
U8 = mybir.dt.uint8
U32 = mybir.dt.uint32
I32 = mybir.dt.int32

GROUP = 512
BLOCKS = GROUP // P
SEG = 8
CHUNK = 8
HALF = 8
ON = 0x40
F16_TOP = 2.0 ** 15
BIG = 1e30
F1_RANGE = 2.0 ** 4
D_TOP = 1e7
WH_LEAST = 0.125
LOADS = 2 * SEG // HALF
AHEAD = 6
SLOTS = 4
SUMS_AT = 3
TILT = ((3, 7), (3, 7))
LOW = 7


def bit_of(g):
    return g % LOW if g < 2 * LOW else 7


def byte_of(g):
    return g - 2 * LOW if isinstance(g, int) and g >= 2 * LOW else g // LOW


def load_adj(pool, adj, adjb, adj_in, g, s, h):
    adj_t = adj.rearrange("(g b p) j -> g p b j", p=P, b=BLOCKS)
    n = s * LOADS + h
    slot = n % SLOTS
    pool.dma_start(adjb[:, slot], adj_t[g, :, :, n * (HALF * P):(n + 1) * (HALF * P)]).then_inc(adj_in[slot], 16)


def build(nc, x, adj, w0, a0, w1, a1, out):
    N, F = x.shape
    JB = N // P
    NG = N // GROUP
    PAIRS = JB // 2
    SEGS = PAIRS // SEG
    CH = JB // CHUNK
    E = F + 1
    GC = 2 * E
    assert F == 64 and NG % 8 == 0 and PAIRS % SEG == 0

    x1 = nc.dram_tensor("x_after_layer0", [N, F], F32, kind="Internal").ap()

    with ExitStack() as ctx:
        def sb(name, shape, dt, c=ctx):
            return c.enter_context(nc.sbuf_tensor(name, shape, dt))

        packed = sb("packed", [P, JB, (NG // 8) * GROUP], U8)
        srow = sb("srow", [P, N], F32)
        G_flat = sb("G", [P, JB * 2 * GC], F16)
        ident = sb("ident", [P, P], F32)
        identb = sb("identb", [P, P], BF16)
        negd = sb("negd", [P, JB], F32)
        scol = sb("scol", [P, JB], F32)
        wh = sb("wh", [P, JB, F], F32)
        alpha = sb("alpha", [P, JB], F32)
        beta = sb("beta", [P, JB], F32)
        csum = sb("csum", [P, F], F32)
        bigd = sb("bigd", [P, JB], F32)
        fast = sb("fast", [P, 2], F32)
        fast_int = sb("fast_int", [P, 2], I32)
        to_bit = sb("to_bit", [P, NG], U32)
        to_on = sb("to_on", [P, NG], U32)

        adjb = sb("adjb", [P, SLOTS, BLOCKS, HALF * P], BF16)
        adj_in = [nc.alloc_semaphore(f"adj_in{i}") for i in range(SLOTS)]

        cleared = []

        def clear(sems):
            for semaphore in sems:
                nc.gpsimd.sem_clear(semaphore)
            for semaphore in cleared:
                nc.release_semaphore(semaphore)
            cleared[:] = sems

        clear(constants(nc, ident, identb, to_bit, to_on))
        for layer, (src, w, a, dst) in enumerate(((x, w0, a0, x1), (x1, w1, a1, out))):
            clear(prologue(nc, layer, src, w, a, srow, G_flat, ident, negd, bigd, scol, wh, alpha, beta, csum,
                           fast, fast_int, packed, adj, adjb, adj_in))
            clear(main(nc, layer, src, adj, dst, packed, srow, G_flat, identb, negd, bigd, alpha, beta, csum,
                       to_bit, to_on, fast_int, adjb, adj_in))
            clear(general(nc, layer, src, adj, dst, packed, srow, ident, negd, scol, wh, csum, fast_int, adjb, adj_in))


def constants(nc, ident, identb, to_bit, to_on):
    with ExitStack() as ctx:
        zeroed = nc.alloc_semaphore("ident_zeroed")
        made = nc.alloc_semaphore("ident_made")
        block = ctx.enter_context(nc.Block())

        @block.gpsimd
        def _(pool):
            nc.gpsimd.memset(ident[:], 0.0).then_inc(zeroed, 1)
            pool.wait_ge(zeroed, 1)
            nc.gpsimd.affine_select(out=ident[:], in_=ident[:], compare_op=ALU.not_equal, fill=1.0, base=0,
                                    pattern=[[-1, P]], channel_multiplier=1).then_inc(made, 1)
            for g in range(to_bit.shape[1]):
                nc.gpsimd.memset(to_bit[:, g:g + 1], bit_of(g))
                nc.gpsimd.memset(to_on[:, g:g + 1], max(6 - bit_of(g), 0))

        @block.vector
        def _(dve):
            dve.wait_ge(made, 1)
            nc.vector.tensor_copy(identb[:], ident[:])
    return [zeroed, made]


def prologue(nc, layer, src, w, a, srow, G_flat, ident, negd, bigd, scol, wh, alpha, beta, csum, fast, fast_int,
             packed, adj, adjb, adj_in):
    N, F = src.shape
    JB = N // P
    CH = JB // CHUNK
    E = F + 1
    T = CHUNK * P
    src_t = src.rearrange("(n p) f -> p n f", p=P)
    G = G_flat[:].rearrange("p (n c t e) -> p n c t e", c=2, t=2, e=E)
    L = f"{layer}"
    with ExitStack() as ctx:
        def sb(name, shape, dt=F32):
            return ctx.enter_context(nc.sbuf_tensor(name + L, shape, dt))

        def ps(name, shape, dt=F32):
            return ctx.enter_context(nc.psum_tensor(name + L, shape, dt))

        sems = []

        def sem(name):
            sems.append(nc.alloc_semaphore(name + L))
            return sems[-1]

        F2 = 2 * F
        wstack = sb("wstack", [F2, F])
        wside = sb("wside", [F, F2])
        acols = sb("acols", [F, 2])
        wblk = sb("wblk", [F2, 2 * (F + 2)])
        mhalf = sb("mhalf", [P, CHUNK])
        maxes = sb("maxes", [P, CH])
        most = sb("most", [P, 3])
        top = sb("top", [P, 3])
        ref = sb("ref", [P, 4])
        spread = sb("spread", [P, 2])
        fits = sb("fits", [P, 5])
        xc = sb("xc", [P, 2, CHUNK, F])
        rows = sb("rows", [P, 5, CHUNK, F])
        xm, sq = rows[:, 0:3], rows[:, 3:5]
        hn = sb("hn", [P, 2, CHUNK, F])
        hT = sb("hT", [F2, T // 2])
        stats = sb("stats", [P, CH, 5, CHUNK])
        fexp = sb("fexp", [P, 2, JB])
        fcol = sb("fcol", [P, 2, JB])
        gf = rows[:].rearrange("p a n f -> p (a n f)")[:, 0:4 * CHUNK * E].rearrange("p (w k m) -> p w k m", w=2, k=2)
        hsum = sb("hsum", [F2, CH])
        hs1 = sb("hs1", [F2, 1])
        hsrep = sb("hsrep", [F2, P])
        tcol = sb("tcol", [P, 3, JB])

        psW = ps("psW", [P, 512])
        psT = ps("psT", [F2, T // 2])
        psS = ps("psS", [P, T])
        psWh = ps("psWh", [P, 4, 512])

        w_in = sem("w_in")
        consts_set = sem("consts_set")
        blk_zeroed = sem("blk_zeroed")
        w_turned = sem("w_turned")
        w_ready = sem("w_ready")
        wa_done = sem("wa_done")
        wblk_ready = sem("wblk_ready")
        x_in = [sem("x_in_a"), sem("x_in_b")]
        dve_step = sem("dve_step")
        centred = sem("centred")
        squared = sem("squared")
        var_ready = sem("var_ready")
        rstd_ready = sem("rstd_ready")
        hn_ready = sem("hn_ready")
        turned = sem("turned")
        hT_ready = sem("hT_ready")
        s_ready = sem("s_ready")
        s_done = sem("s_done")
        s_copied = sem("s_copied")
        wh_done = sem("wh_done")
        wh_copied = sem("wh_copied")
        cols_copied = sem("cols_copied")
        most_ready = sem("most_ready")
        top_ready = sem("top_ready")
        ref_ready = sem("ref_ready")
        f_ready = sem("f_ready")
        f_scaled = sem("f_scaled")
        spread_ready = sem("spread_ready")
        spread_exp = sem("spread_exp")
        gf_ready = [sem("gf_ready_dve"), sem("gf_ready_pool")]
        hi_ready = [sem("hi_ready_dve"), sem("hi_ready_pool")]
        lo_ready = [sem("lo_ready_dve"), sem("lo_ready_pool")]
        hsum_ready = sem("hsum_ready")
        csum_done = sem("csum_done")
        exps_in = sem("exps_in")
        block = ctx.enter_context(nc.Block())
        banks = psWh[:, :, 0:4 * (F + 2)].rearrange("p b (n e) -> p b n e", e=F + 2)

        def wh_banks(q):
            return banks[:, q % 2 * 2:q % 2 * 2 + 2]

        def part_of(q, c, part):
            return G[:, q * CHUNK:(q + 1) * CHUNK, c, part, :]

        def blocks(t):
            return t.rearrange("p (n e) -> p n e", e=E)

        pieces = [(q, c) for q in range(CH) for c in range(2)]
        shares = [[p for n, p in enumerate(pieces) if n % 3 < 2], [p for n, p in enumerate(pieces) if n % 3 == 2]]

        def split(eng, who):
            e = nc.vector if who == 0 else nc.gpsimd
            mine = shares[who]

            def product(k):
                q, c = mine[k]
                cols = slice(q * CHUNK, (q + 1) * CHUNK)
                buf = blocks(gf[:, who, k % 2])
                if k >= 2:
                    eng.wait_ge(lo_ready[who], k - 1)
                e.tensor_tensor(buf[:, :, 0:F], wh[:, cols, :],
                                fcol[:, c, cols].unsqueeze(2).broadcast_to([P, CHUNK, F]), ALU.mult)
                e.tensor_copy(buf[:, :, F:E], fcol[:, c, cols].unsqueeze(2)).then_inc(gf_ready[who], 1)

            eng.wait_ge(f_scaled, 2)
            product(0)
            for k in range(len(mine)):
                if k + 1 < len(mine):
                    product(k + 1)
                q, c = mine[k]
                eng.wait_ge(gf_ready[who], k + 1)
                eng.wait_ge(hi_ready[who], k + 1)
                e.tensor_tensor(part_of(q, c, 1), blocks(gf[:, who, k % 2]), part_of(q, c, 0),
                                ALU.subtract).then_inc(lo_ready[who], 1)

        @block.sync
        def _(sp):
            if layer == 0:
                sp.dma_start(wstack[0:F, :], w).then_inc(w_in, 16)
                sp.dma_start(wstack[F:F2, :], w).then_inc(w_in, 16)
            else:
                sp.dma_start(wside[:, 0:F], w).then_inc(w_in, 16)
                sp.dma_start(wside[:, F:F2], w).then_inc(w_in, 16)
            av = a.rearrange("(t f) o -> f (t o)", t=2) if len(a.shape) == 2 else a.rearrange("(t f) -> f t", t=2)
            with nc.allow_non_contiguous_dma("128 floats"):
                sp.dma_start(acols[:], av).then_inc(w_in, 16)
            for q in range(CH):
                if q >= 2:
                    sp.wait_ge(centred, q - 1)
                sp.dma_start(xc[:, q % 2], src_t[:, q * CHUNK:(q + 1) * CHUNK, :]).then_inc(x_in[q % 2], 16)

        @block.gpsimd
        def _(pool):
            nc.gpsimd.memset(wblk[:], 0.0).then_inc(blk_zeroed, 1)
            if layer == 0:
                for n in range(SLOTS):
                    load_adj(pool, adj, adjb, adj_in, 0, n // LOADS, n % LOADS)
            nc.gpsimd.memset(mhalf[:], -0.5).then_inc(consts_set, 1)
            pool.wait_ge(consts_set, 1)
            for q in range(CH):
                pool.wait_ge(var_ready, q + 1)
                nc.gpsimd.tensor_tensor(stats[:, q, 4, :], stats[:, q, 3, :], mhalf[:], ALU.pow).then_inc(rstd_ready, 1)
                if layer == 0:
                    words = packed[:].rearrange("p a b -> p (a b)").bitcast(U32)
                    size = words.shape[1] // CH
                    nc.gpsimd.memset(words[:, q * size:(q + 1) * size], 0)
            pool.wait_ge(most_ready, 1)
            nc.gpsimd.partition_all_reduce(top[:], most[:], P, bass.bass_isa.ReduceOp.max).then_inc(top_ready, 1)
            split(pool, 1)

        @block.scalar
        def _(act):
            for t in range(CH + 3):
                q = t
                if q < CH:
                    act.wait_ge(centred, q + 1)
                    if q >= 2:
                        act.wait_ge(var_ready, q - 1)
                    nc.scalar.activation(sq[:, q % 2], xm[:, q % 3], ACT.Square).then_inc(squared, 1)
                q = t - 2
                if 0 <= q < CH:
                    act.wait_ge(turned, q + 1)
                    if q >= 1:
                        act.wait_ge(wh_done, q)
                    nc.scalar.activation(hT[:], psT[:], ACT.Relu, accum_out=hsum[:, q:q + 1]).then_inc(hT_ready, 1)
                q = t - 3
                if q >= 0:
                    act.wait_ge(cols_copied, q + 1)
                    nc.scalar.copy(wh[:, q * CHUNK:(q + 1) * CHUNK, :].rearrange("p (b n) f -> p b n f", b=2),
                                   wh_banks(q)[:, :, :, 0:F]).then_inc(wh_copied, 1)
                    act.wait_ge(s_done, q + 1)
                    nc.scalar.copy(srow[:, q * T:(q + 1) * T], psS[:]).then_inc(s_copied, 1)
            act.wait_ge(ref_ready, 1)
            nc.scalar.activation(fexp[:, 0, :], negd[:], ACT.Exp, bias=ref[:, 0:1], scale=-1.0).then_inc(f_ready, 1)
            nc.scalar.activation(fexp[:, 1, :], negd[:], ACT.Exp, bias=ref[:, 1:2], scale=-0.2).then_inc(f_ready, 1)
            act.wait_ge(spread_ready, 1)
            nc.scalar.activation(spread[:, 1:2], spread[:, 0:1], ACT.Exp).then_inc(spread_exp, 1)
            act.wait_ge(exps_in, 2)
            nc.scalar.activation(alpha[:], tcol[:, 1, :], ACT.Exp)
            nc.scalar.activation(beta[:], tcol[:, 2, :], ACT.Exp)
            for q, c in pieces:
                who = 0 if (q, c) in shares[0] else 1
                k = shares[who].index((q, c))
                act.wait_ge(gf_ready[who], k + 1)
                nc.scalar.copy(part_of(q, c, 0), blocks(gf[:, who, k % 2])).then_inc(hi_ready[who], 1)

        @block.tensor
        def _(pe):
            pe.wait_ge(w_in, 48)
            if layer == 0:
                nc.tensor.transpose(psW[0:F, 0:F2], wstack[:], ident[:]).then_inc(w_turned, 1)
            else:
                nc.tensor.transpose(psW[0:F2, 0:F], wside[:], ident[0:F, 0:F]).then_inc(w_turned, 1)
            pe.wait_ge(w_ready, 1)
            nc.tensor.matmul(psW[0:F2, 128:130], wside[:], acols[:], start=True, stop=True).then_inc(wa_done, 1)
            pe.wait_ge(wblk_ready, 6)
            for q in range(CH + 1):
                if q < CH:
                    pe.wait_ge(hn_ready, q + 1)
                    if q >= 1:
                        pe.wait_ge(hT_ready, q)
                    for n in range(CHUNK // 2):
                        t = nc.tensor.transpose(psT[:, n * P:(n + 1) * P],
                                                hn[:, q % 2, 2 * n:2 * n + 2, :].rearrange("p n f -> p (n f)"),
                                                ident[:])
                    t.then_inc(turned, 1)
                if q >= 1:
                    pe.wait_ge(s_ready, q)
                    if q >= 2:
                        pe.wait_ge(s_copied, q - 1)
                    for n in range(CHUNK):
                        jb = (q - 1) * CHUNK + n
                        m = nc.tensor.matmul(psS[:, n * P:(n + 1) * P], scol[:, jb:jb + 1].broadcast_to([P, P]),
                                             ident[:], start=True, stop=True)
                    m.then_inc(s_done, 1)
                if q < CH:
                    pe.wait_ge(hT_ready, q + 1)
                    if q >= 2:
                        pe.wait_ge(wh_copied, q - 1)
                    for n in range(CHUNK // 2):
                        o = n % 2 * 2 * (F + 2)
                        m = nc.tensor.matmul(psWh[:, q % 2 * 2 + n // 2, o:o + 2 * (F + 2)],
                                             hT[:, n * P:(n + 1) * P], wblk[:], start=True, stop=True)
                    m.then_inc(wh_done, 1)
            pe.wait_ge(hsum_ready, 1)
            nc.tensor.matmul(psW[:, 0:F], hsrep[:], wstack[:], start=True, stop=True).then_inc(csum_done, 1)

        @block.vector
        def _(dve):
            steps = [0]

            def then(ins):
                steps[0] += 1
                ins.then_inc(dve_step, 1)
                dve.wait_ge(dve_step, steps[0])

            def centre(q):
                xq = xc[:, q % 2]
                dve.wait_ge(x_in[q % 2], 16 * (q // 2 + 1))
                then(nc.vector.tensor_reduce(stats[:, q, 0, :], xq, AX.X, ALU.add))
                then(nc.vector.tensor_scalar(stats[:, q, 1, :], stats[:, q, 0, :], -1.0 / F, None, ALU.mult))
                if q >= 3:
                    dve.wait_ge(hn_ready, q - 2)
                nc.vector.tensor_tensor(xm[:, q % 3], xq, stats[:, q, 1, :].unsqueeze(2).broadcast_to([P, CHUNK, F]),
                                        ALU.add).then_inc(centred, 1)

            def variance(q):
                dve.wait_ge(squared, q + 1)
                then(nc.vector.tensor_reduce(stats[:, q, 2, :], sq[:, q % 2], AX.X, ALU.add))
                nc.vector.tensor_scalar(stats[:, q, 3, :], stats[:, q, 2, :], 1.0 / F, 1e-5, ALU.mult,
                                        ALU.add).then_inc(var_ready, 1)

            def normed(q):
                dve.wait_ge(rstd_ready, q + 1)
                if q >= 2:
                    dve.wait_ge(turned, q - 1)
                nc.vector.tensor_tensor(hn[:, q % 2], xm[:, q % 3],
                                        stats[:, q, 4, :].unsqueeze(2).broadcast_to([P, CHUNK, F]),
                                        ALU.mult).then_inc(hn_ready, 1)

            def columns(q):
                dve.wait_ge(wh_done, q + 1)
                cols = slice(q * CHUNK, (q + 1) * CHUNK)

                def two(t):
                    return t.rearrange("p (b n) -> p b n", b=2)
                nc.vector.tensor_copy(two(scol[:, cols]), wh_banks(q)[:, :, :, F + 1]).then_inc(s_ready, 1)
                nc.vector.tensor_scalar(two(bigd[:, cols]), wh_banks(q)[:, :, :, F], BIG, None, ALU.mult)
                nc.vector.tensor_scalar(two(negd[:, cols]), wh_banks(q)[:, :, :, F], -1.0, None,
                                        ALU.mult).then_inc(cols_copied, 1)

            def largest(q):
                dve.wait_ge(wh_copied, q + 1)
                nc.vector.tensor_reduce(maxes[:, q:q + 1], wh[:, q * CHUNK:(q + 1) * CHUNK, :], AX.XY, ALU.max,
                                        apply_absolute_value=True)

            dve.wait_ge(w_in, 48)
            dve.wait_ge(blk_zeroed, 1)
            dve.wait_ge(w_turned, 1)
            if layer == 0:
                nc.vector.tensor_copy(wside[:], psW[0:F, 0:F2]).then_inc(w_ready, 1)
            else:
                nc.vector.tensor_copy(wstack[:], psW[0:F2, 0:F]).then_inc(w_ready, 1)
            dve.wait_ge(w_ready, 1)
            dve.wait_ge(wa_done, 1)
            for r in range(2):
                rows, o = slice(r * F, (r + 1) * F), r * (F + 2)
                nc.vector.tensor_copy(wblk[rows, o:o + F], wstack[rows, :]).then_inc(wblk_ready, 1)
                nc.vector.tensor_copy(wblk[rows, o + F:o + F + 1], psW[rows, 129:130]).then_inc(wblk_ready, 1)
                nc.vector.tensor_copy(wblk[rows, o + F + 1:o + F + 2], psW[rows, 128:129]).then_inc(wblk_ready, 1)
            for t in range(CH + 4):
                if t < CH:
                    centre(t)
                if 0 <= t - 1 < CH:
                    variance(t - 1)
                if 0 <= t - 2 < CH:
                    normed(t - 2)
                if 0 <= t - 3 < CH:
                    columns(t - 3)
                if 0 <= t - 4:
                    largest(t - 4)
            dve.wait_ge(cols_copied, CH)
            nc.vector.tensor_reduce(most[:, 1:2], negd[:], AX.X, ALU.max)
            then(nc.vector.tensor_reduce(most[:, 0:1], negd[:], AX.X, ALU.min))
            nc.vector.tensor_scalar(most[:, 0:1], most[:, 0:1], -1.0, None, ALU.mult)
            nc.vector.tensor_reduce(most[:, 2:3], maxes[:], AX.X, ALU.max).then_inc(most_ready, 1)
            dve.wait_ge(top_ready, 1)
            nc.vector.tensor_scalar(ref[:, 1:2], top[:, 0:1], -0.2, None, ALU.mult)
            then(nc.vector.tensor_scalar(ref[:, 2:3], top[:, 2:3], 1.0, 1.0 / F16_TOP, ALU.max, ALU.mult))
            nc.vector.tensor_scalar(ref[:, 0:1], top[:, 0:1], -1.0, None, ALU.mult).then_inc(ref_ready, 1)
            nc.vector.tensor_tensor(spread[:, 0:1], top[:, 0:1], top[:, 1:2], ALU.add).then_inc(spread_ready, 1)
            then(nc.vector.reciprocal(ref[:, 3:4], ref[:, 2:3]))
            then(nc.vector.tensor_scalar(tcol[:, 0, :], scol[:], top[:, 0:1], 0.8, ALU.add, ALU.mult))
            nc.vector.tensor_scalar(tcol[:, 1, :], tcol[:, 0, :], 0.0, None, ALU.min).then_inc(exps_in, 1)
            nc.vector.tensor_scalar(tcol[:, 2, :], tcol[:, 0, :], -1.0, 0.0, ALU.mult, ALU.min).then_inc(exps_in, 1)
            dve.wait_ge(f_ready, 2)
            for c in range(2):
                nc.vector.tensor_scalar(fcol[:, c, :], fexp[:, c, :], ref[:, 3:4], None, ALU.mult).then_inc(f_scaled, 1)
            split(dve, 0)
            dve.wait_ge(hT_ready, CH)
            then(nc.vector.tensor_reduce(hs1[:], hsum[:], AX.X, ALU.add))
            nc.vector.tensor_copy(hsrep[:], hs1[:, 0:1].broadcast_to([F2, P])).then_inc(hsum_ready, 1)
            dve.wait_ge(csum_done, 1)
            nc.vector.tensor_copy(csum[:], psW[:, 0:F])
            dve.wait_ge(spread_exp, 1)
            then(nc.vector.tensor_tensor(fits[:, 4:5], spread[:, 1:2], ref[:, 2:3], ALU.mult))
            nc.vector.tensor_scalar(fits[:, 0:1], fits[:, 4:5], F1_RANGE, None, ALU.is_le)
            nc.vector.tensor_scalar(fits[:, 1:3], top[:, 0:2], D_TOP, None, ALU.is_le)
            then(nc.vector.tensor_scalar(fits[:, 3:4], top[:, 2:3], WH_LEAST, None, ALU.is_ge))
            if layer == 1:
                then(nc.vector.tensor_tensor(fits[:, 3:4], fits[:, 3:4], fast[:, 0:1], ALU.mult))
            then(nc.vector.tensor_reduce(fast[:, layer:layer + 1], fits[:, 0:4], AX.X, ALU.min))
            nc.vector.tensor_copy(fast_int[:, layer:layer + 1], fast[:, layer:layer + 1])

    return sems


def main(nc, layer, src, adj, dst, packed, srow, G_flat, identb, negd, bigd, alpha, beta, csum, to_bit, to_on,
         fast_int, adjb, adj_in):
    N, F = src.shape
    JB = N // P
    NG = N // GROUP
    PAIRS = JB // 2
    SEGS = PAIRS // SEG
    E = F + 1
    GC = 2 * E
    W2 = 2 * GROUP
    PPH = HALF // 2
    RING = SLOTS if layer == 0 else 2 * SLOTS
    assert SLOTS % LOADS == 0 and SEGS * LOADS % SLOTS == 0 and SEG % SLOTS == 0 and SEG % RING == 0
    L = f"{layer}"
    src_t = src.rearrange("(g b p) f -> g p b f", p=P, b=BLOCKS)
    dst_t = dst.rearrange("(g b p) f -> g p b f", p=P, b=BLOCKS)
    with ExitStack() as ctx:
        def sb(name, shape, dt=F32):
            return ctx.enter_context(nc.sbuf_tensor(name + L, shape, dt))

        sems = []

        def sem(name):
            sems.append(nc.alloc_semaphore(name + L))
            return sems[-1]

        m01 = sb("m01", [P, SLOTS, W2], U8) if layer == 0 else None
        def ring(name, n):
            if layer == 0:
                return sb(name, [P, RING, W2], U8)
            tiles = adjb[:].rearrange("p s b j -> p (s b j)").bitcast(U8)
            return tiles[:, n * RING * W2:(n + 1) * RING * W2].rearrange("p (k m) -> p k m", k=RING)

        mon = ring("mon", 0)
        c1 = ring("c1", 1)
        a1 = ring("a1", 2)
        a2 = ring("a2", 3)
        R = sb("R", [P, BLOCKS, 2, E])
        nd = sb("nd", [P, BLOCKS, E])
        v = sb("v", [P, BLOCKS, F])
        neg = sb("neg", [P, BLOCKS, F])
        ex = sb("ex", [P, BLOCKS, F])
        xg = sb("xg", [P, BLOCKS, F])
        small = sb("small", [P, 4, BLOCKS])
        acc = ctx.enter_context(nc.psum_tensor("acc" + L, [P, BLOCKS, 512], F32))
        tp = ctx.enter_context(nc.psum_tensor("tp" + L, [P, SLOTS, W2], BF16)) if layer == 0 else None

        turned = sem("turned_pairs")
        m01_ready = sem("m01_ready")
        m01_packed = sem("m01_packed")
        mon_ready = sem("mon_ready")
        c1_dve = sem("c1_dve")
        c1_act = sem("c1_act")
        a1_ready = sem("a1_ready")
        a2_ready = sem("a2_ready")
        pairs_done = sem("pairs_done")
        blocks_done = sem("blocks_done")
        sums_read = sem("sums_read")
        pool_step = sem("pool_step")
        scaled = sem("scaled")
        v_ready = sem("v_ready")
        neg_ready = sem("neg_ready")
        exp_done = sem("exp_done")
        finish_step = sem("finish_step")
        ex_ready = sem("ex_ready")
        out_ready = sem("out_ready")
        xg_in = sem("xg_in")
        stored = sem("stored")
        small_set = sem("small_set")
        pe_passed = sem("pe_passed")
        pool_passed = sem("pool_passed")
        act_passed = sem("act_passed")
        block = ctx.enter_context(nc.Block())

        def u32(t):
            return t.bitcast(U32)

        def pair(g, s, i):
            return g * PAIRS + s * SEG + i

        def act_blocks(i):
            if i in TILT[layer]:
                return () if layer == 0 else (0, 1)
            return (1,)

        def count(g, s, i, skipped):
            return (g * SEGS + s) * (SEG - len(skipped)) + len([j for j in range(i) if j not in skipped])

        def by_act(g, s, i):
            return count(g, s, i, TILT[0] if layer == 0 else ())

        def by_dve(g, s, i):
            return count(g, s, i, () if layer == 0 else TILT[1])

        def wait_past(eng, semaphore, value, first):
            if not first or value > 0:
                eng.wait_ge(semaphore, value)

        def groups(eng, body, looped=NG - 1):
            with eng.If(eng.value_load(fast_int[0:1, layer:layer + 1], min_val=0, max_val=1) > 0):
                body(0, True, False)
                with eng.Fori(1, looped) as g:
                    body(g, False, False)
                for g in range(looped, NG):
                    body(g, False, g == NG - 1)

        STEPS = 8

        def spread(t, n):
            return t.unsqueeze(2).broadcast_to([P, BLOCKS, n])

        def output_steps(e, inverse):
            tt, ts = e.tensor_tensor, e.tensor_scalar
            return [
                lambda: tt(nd[:], R[:, :, 0, :], R[:, :, 1, :], ALU.add),
                lambda: ts(small[:, 0, :], nd[:, :, F], 0.0, None, ALU.is_equal),
                lambda: ts(small[:, 1, :], small[:, 0, :], float(N), None, ALU.mult),
                lambda: tt(small[:, 1, :], small[:, 1, :], nd[:, :, F], ALU.add),
                lambda: inverse(small[:, 2, :], small[:, 1, :]),
                lambda: tt(v[:], spread(small[:, 0, :], F), csum[:].unsqueeze(1).broadcast_to([P, BLOCKS, F]),
                           ALU.mult),
                lambda: tt(v[:], v[:], nd[:, :, 0:F], ALU.add),
                lambda: tt(v[:], v[:], spread(small[:, 2, :], F), ALU.mult),
                lambda: tt(v[:], v[:], neg[:], ALU.add),
                lambda: tt(v[:], v[:], ex[:], ALU.add),
                lambda: tt(xg[:], v[:], xg[:], ALU.add),
            ]

        @block.gpsimd
        def _(pool):
            nc.gpsimd.memset(small[:, 3, :], -1.0).then_inc(small_set, 1)
            pool.wait_ge(small_set, 1)
            def power(out, x):
                return nc.gpsimd.tensor_tensor(out, x, small[:, 3, :], ALU.pow)

            def output_step(g, k):
                if k == 0:
                    pool.wait_ge(scaled, g + 1)
                else:
                    pool.wait_ge(pool_step, g * (STEPS + 2) + k)
                if k == STEPS:
                    pool.wait_ge(ex_ready, g + 1)
                elif k == STEPS + 2:
                    pool.wait_ge(xg_in, 16 * (g + 1))
                    output_steps(nc.gpsimd, power)[k]().then_inc(out_ready, 1)
                    return
                pool.sem_inc(pool_passed, 1)
                output_steps(nc.gpsimd, power)[k]().then_inc(pool_step, 1)
                if k == STEPS - 1:
                    pool.wait_ge(pool_step, g * (STEPS + 2) + STEPS)
                    pool.sem_inc(v_ready, 1)

            def reload(g, s, i, last):
                s1 = s + SLOTS // LOADS
                if last and s1 >= SEGS:
                    return
                pool.wait_ge(turned, pair(g, s, i + PPH))
                load_adj(pool, adj, adjb, adj_in, g + s1 // SEGS, s1 % SEGS, i // PPH)

            def segment(g, s, last, steps=()):
                for i in range(SEG):
                    k = i % RING
                    pool.wait_ge(a1_ready, pair(g, s, i + 1))
                    nc.gpsimd.tensor_tensor(u32(a2[:, k]), u32(mon[:, k]), u32(a1[:, k]),
                                            ALU.subtract).then_inc(a2_ready, 1)
                    if layer == 0 and i % PPH == 0:
                        reload(g, s, i, last)
                    if i < len(steps):
                        output_step(g - 1, steps[i])

            def body(g, first, last):
                segment(g, 0, last)
                segment(g, 1, last, () if first else range(STEPS))
                segment(g, 2, last)
                segment(g, 3, last, () if first else range(STEPS, STEPS + 3))

            assert SEGS == 4
            groups(pool, body)

        @block.sync
        def _(sp):
            def store(g):
                sp.wait_ge(out_ready, g + 1)
                sp.dma_start(dst_t[g], xg[:]).then_inc(stored, 16)

            def body(g, first, last):
                if not first:
                    store(g - 1)
                    sp.wait_ge(stored, 16 * g)
                sp.dma_start(xg[:], src_t[g]).then_inc(xg_in, 16)
                if last:
                    store(g)
                    sp.wait_ge(stored, 16 * NG)

            groups(sp, body)

        @block.scalar
        def _(act):
            def segment(g, s, first):
                for i in range(SEG):
                    k = i % RING
                    if act_blocks(i):
                        wait_past(act, a1_ready, pair(g, s, i + 1 - RING), first)
                        if not first or i >= RING:
                            act.sem_inc(act_passed, 1)
                        for n in act_blocks(i):
                            r = nc.scalar.activation(
                                c1[:, k, n * GROUP:(n + 1) * GROUP], srow[:, bass.ds(g * GROUP, GROUP)], ACT.Relu,
                                bias=bigd[:, bass.ds(s * (2 * SEG) + 2 * i + n, 1)], scale=BIG)
                        r.then_inc(c1_act, 1)
                    if layer == 0:
                        act.wait_ge(turned, pair(g, s, i + 1))
                        wait_past(act, m01_packed, pair(g, s, i + 1 - RING), first)
                        nc.scalar.activation(m01[:, k], tp[:, k], ACT.Sign).then_inc(m01_ready, 1)

            def exp_of(g):
                act.wait_ge(v_ready, g + 1)
                nc.scalar.activation(neg[:], v[:], ACT.Relu, scale=-1.0).then_inc(neg_ready, 1)
                act.wait_ge(neg_ready, g + 1)
                nc.scalar.activation(ex[:], neg[:], ACT.Exp, scale=-1.0).then_inc(exp_done, 1)
                act.wait_ge(exp_done, g + 1)
                nc.scalar.activation(ex[:], ex[:], ACT.Copy, bias=-1.0).then_inc(ex_ready, 1)

            def scale_sums(g):
                act.wait_ge(sums_read, (g + 1) * BLOCKS)
                act.sem_inc(act_passed, 1)
                for b in range(BLOCKS):
                    for which, factor in ((0, alpha), (1, beta)):
                        r = nc.scalar.activation(R[:, b, which, :], R[:, b, which, :], ACT.Copy,
                                                 scale=factor[:, bass.ds(g * BLOCKS + b, 1)])
                r.then_inc(scaled, 1)

            def body(g, first, last):
                segment(g, 0, first)
                if not first:
                    scale_sums(g - 1)
                with act.Fori(1, SEGS - 1) as s:
                    segment(g, s, False)
                if not first:
                    exp_of(g - 1)
                segment(g, SEGS - 1, False)
                if last:
                    exp_of(g)

            groups(act, body)

        @block.tensor
        def _(pe):
            def turn(g, s, i, first):
                if i >= SEG:
                    s, i, first = s + 1, i - SEG, False
                k = i % RING
                n_load = s * LOADS + i // PPH
                slot = n_load % SLOTS
                if i % PPH == 0:
                    pe.wait_ge(adj_in[slot], 16 * (g * (SEGS * LOADS // SLOTS) + n_load // SLOTS + 1))
                wait_past(pe, m01_ready, pair(g, s, i + 1 - RING), first)
                for n in range(2):
                    for b in range(BLOCKS):
                        j = (2 * i + n) % HALF
                        t = nc.tensor.transpose(tp[:, k, n * GROUP + b * P:n * GROUP + (b + 1) * P],
                                                adjb[:, slot, b, j * P:(j + 1) * P], identb[:])
                t.then_inc(turned, 1)

            def products(g, s, i, opening, closing, first):
                k = i % RING
                pe.wait_ge(a1_ready, pair(g, s, i + 1))
                pe.wait_ge(a2_ready, pair(g, s, i + 1))
                pe.sem_inc(pe_passed, 1)
                for b in range(BLOCKS):
                    if opening and not first:
                        pe.wait_ge(sums_read, (g - 1) * BLOCKS + b + 1)
                        pe.sem_inc(pe_passed, 1)
                    for n in range(2):
                        for which, tile in ((0, a1), (1, a2)):
                            at = ((s * 2 * SEG + 2 * i + n) * 2 + which) * GC
                            q = nc.tensor.matmul(
                                acc[:, b, which * GC:(which + 1) * GC],
                                tile[:, k, n * GROUP + b * P:n * GROUP + (b + 1) * P].bitcast(FP8),
                                G_flat[:, at:at + GC],
                                start=(opening and n == 0 and which == 0), stop=False, skip_group_check=True)
                    if closing and b < BLOCKS - 1:
                        q.then_inc(blocks_done, 1)
                q.then_inc(pairs_done, 1)

            def segment(g, s, first, opening, closing, last):
                for i in range(SEG):
                    if layer == 0 and not (closing and last and i + AHEAD >= SEG):
                        turn(g, s, i + AHEAD, first)
                    products(g, s, i, opening and i == 0, closing and i == SEG - 1, first)

            def body(g, first, last):
                if first and layer == 0:
                    for i in range(AHEAD):
                        turn(g, 0, i, True)
                for s in range(SEGS):
                    segment(g, s, first and s == 0, s == 0, s == SEGS - 1, last)

            groups(pe, body)

        @block.vector
        def _(dve):
            def sums(g):
                if not isinstance(g, int) or g > 0:
                    dve.wait_ge(out_ready, g)
                for b in range(BLOCKS):
                    if b < BLOCKS - 1:
                        dve.wait_ge(blocks_done, g * (BLOCKS - 1) + b + 1)
                    else:
                        dve.wait_ge(pairs_done, (g + 1) * PAIRS)
                    nc.vector.tensor_reduce(
                        R[:, b], acc[:, b, 0:2 * GC].rearrange("p (c t e) -> p c e t", c=2, t=2), AX.X,
                        ALU.add).then_inc(sums_read, 1)

            def finish(g):
                done = [0]

                def then(ins):
                    done[0] += 1
                    ins.then_inc(finish_step, 1)
                    dve.wait_ge(finish_step, done[0])

                dve.wait_ge(sums_read, (g + 1) * BLOCKS)
                for which, factor in ((0, alpha), (1, beta)):
                    then(nc.vector.tensor_tensor(R[:, :, which, :], R[:, :, which, :],
                                                 spread(factor[:, g * BLOCKS:(g + 1) * BLOCKS], E), ALU.mult))
                for k, step in enumerate(output_steps(nc.vector, nc.vector.reciprocal)):
                    if k == STEPS:
                        dve.wait_ge(v_ready, g + 1)
                        dve.wait_ge(ex_ready, g + 1)
                    if k == STEPS + 2:
                        dve.wait_ge(xg_in, 16 * (g + 1))
                        step().then_inc(out_ready, 1)
                    elif k == STEPS - 1:
                        step().then_inc(v_ready, 1)
                    else:
                        then(step())

            def wide(t):
                return u32(t).rearrange("p (n i) -> p n i", n=2)

            def bits(g, s, i):
                return packed[:, bass.ds(s * (2 * SEG) + 2 * i, 2), bass.ds(byte_of(g) * GROUP, GROUP)].bitcast(U32)

            def mask_on(g, s, i, first):
                k = i % RING
                wait_past(dve, a2_ready, pair(g, s, i + 1 - RING), first)
                if layer == 0:
                    dve.wait_ge(m01_ready, pair(g, s, i + 1))
                    nc.vector.tensor_scalar(u32(mon[:, k]), u32(m01[:, k]), 6, None,
                                            ALU.logical_shift_left).then_inc(mon_ready, 1)
                elif isinstance(g, int) and g >= 2 * LOW:
                    nc.vector.tensor_scalar(wide(mon[:, k]), bits(g, s, i), 1, ON * 0x01010101,
                                            ALU.logical_shift_right, ALU.bitwise_and).then_inc(mon_ready, 1)
                else:
                    nc.vector.tensor_scalar(wide(mon[:, k]), bits(g, s, i), to_on[:, bass.ds(g, 1)], ON * 0x01010101,
                                            ALU.logical_shift_left, ALU.bitwise_and).then_inc(mon_ready, 1)

            def compare(g, s, i):
                for n in range(2):
                    if n in act_blocks(i):
                        continue
                    r = nc.vector.tensor_scalar(
                        c1[:, i % RING, n * GROUP:(n + 1) * GROUP], srow[:, bass.ds(g * GROUP, GROUP)],
                        negd[:, bass.ds(s * (2 * SEG) + 2 * i + n, 1)], float(ON), ALU.is_gt, ALU.mult)
                if len(act_blocks(i)) < 2:
                    r.then_inc(c1_dve, 1)

            def pack(g, s, i):
                b = bits(g, s, i)
                nc.vector.scalar_tensor_tensor(b, wide(m01[:, i % RING]), to_bit[:, bass.ds(g, 1)], b,
                                               ALU.logical_shift_left, ALU.bitwise_or).then_inc(m01_packed, 1)

            def and_of(g, s, i, first):
                k = i % RING
                wait_past(dve, pairs_done, pair(g, s, i + 1 - RING), first)
                dve.wait_ge(mon_ready, pair(g, s, i + 1))
                if act_blocks(i):
                    dve.wait_ge(c1_act, by_act(g, s, i + 1))
                if len(act_blocks(i)) < 2:
                    dve.wait_ge(c1_dve, by_dve(g, s, i + 1))
                nc.vector.tensor_tensor(u32(a1[:, k]), u32(mon[:, k]), u32(c1[:, k]),
                                        ALU.bitwise_and).then_inc(a1_ready, 1)

            def segment(g, s, first, between):
                if layer == 1:
                    mask_on(g, s, 0, first)
                for i in range(SEG):
                    if i == SUMS_AT and between:
                        between()
                    if layer == 0:
                        mask_on(g, s, i, first)
                    compare(g, s, i)
                    if layer == 0:
                        pack(g, s, i)
                    elif i + 1 < SEG:
                        mask_on(g, s, i + 1, first)
                    and_of(g, s, i, first)

            def body(g, first, last):
                segment(g, 0, first, None if first else lambda: sums(g - 1))
                with dve.Fori(1, SEGS) as s:
                    segment(g, s, False, None)
                if last:
                    sums(g)
                    finish(g)

            groups(dve, body, 2 * LOW)
    return sems


def general(nc, layer, src, adj, dst, packed, srow, ident, negd, scol, wh, csum, fast_int, adjb, adj_in):
    N, F = src.shape
    JB = N // P
    QUAD = 4
    QUADS = JB // QUAD
    adj_t = adj.rearrange("(t p) j -> t p j", p=P)
    src_t = src.rearrange("(t p) f -> t p f", p=P)
    dst_t = dst.rearrange("(t p) f -> t p f", p=P)
    L = f"{layer}"
    with ExitStack() as ctx:
        def sb(name, shape, dt=F32):
            return ctx.enter_context(nc.sbuf_tensor(name + L, shape, dt))

        sems = []

        def sem(name):
            sems.append(nc.alloc_semaphore("gen_" + name + L))
            return sems[-1]

        spare = packed[:].rearrange("p a b -> p (a b)").bitcast(F32)
        mask, z = spare[:, 0:N], spare[:, N:2 * N]
        nrow = srow
        adjt = adjb[:].rearrange("p s b j -> p (s b j)").bitcast(I32)
        pT = sb("gen_pT", [P, 2, QUAD * P])
        xt = sb("gen_xt", [P, F])
        v = sb("gen_v", [P, F])
        neg = sb("gen_neg", [P, F])
        ex = sb("gen_ex", [P, F])
        few = sb("gen_few", [P, 8])
        psP = ctx.enter_context(nc.psum_tensor("gen_psP" + L, [P, 2, QUAD * P], F32))
        psN = ctx.enter_context(nc.psum_tensor("gen_psN" + L, [P, 512], F32))

        rows_made = sem("rows_made")
        rows_copied = sem("rows_copied")
        adjt_in = sem("adjt_in")
        xt_in = sem("xt_in")
        mask_ready = sem("mask_ready")
        step = sem("step")
        z_ready = sem("z_ready")
        z_exp = sem("z_exp")
        p_ready = sem("p_ready")
        p_turned = sem("p_turned")
        pT_ready = sem("pT_ready")
        quads_done = sem("quads_done")
        neg_ready = sem("neg_ready")
        ex_ready = sem("ex_ready")
        out_ready = sem("out_ready")
        stored = sem("stored")
        block = ctx.enter_context(nc.Block())

        def tiles(eng, body, before=None):
            with eng.If(eng.value_load(fast_int[0:1, layer:layer + 1], min_val=0, max_val=1) < 1):
                if before:
                    before()
                body(0, True)
                with eng.Fori(1, JB) as t:
                    body(t, False)

        @block.sync
        def _(sp):
            def body(t, first):
                if not first:
                    sp.wait_ge(mask_ready, t)
                sp.dma_start(adjt, adj_t[t]).then_inc(adjt_in, 16)
                if not first:
                    sp.wait_ge(xt_in, 16 * t)
                    sp.wait_ge(out_ready, t)
                    sp.dma_start(dst_t[t - 1], xt[:]).then_inc(stored, 16)
                    sp.wait_ge(stored, 16 * t)
                sp.dma_start(xt[:], src_t[t]).then_inc(xt_in, 16)

            with sp.If(sp.value_load(fast_int[0:1, layer:layer + 1], min_val=0, max_val=1) < 1):
                for slot in range(SLOTS):
                    sp.wait_ge(adj_in[slot], 16)
                body(0, True)
                with sp.Fori(1, JB) as t:
                    body(t, False)
                sp.wait_ge(xt_in, 16 * JB)
                sp.wait_ge(out_ready, JB)
                sp.dma_start(dst_t[JB - 1], xt[:]).then_inc(stored, 16)
                sp.wait_ge(stored, 16 * JB)

        @block.tensor
        def _(pe):
            def before():
                for k in range(QUADS):
                    if k >= 2:
                        pe.wait_ge(rows_copied, k - 1)
                    for n in range(QUAD):
                        jb = k * QUAD + n
                        m = nc.tensor.matmul(psP[:, k % 2, n * P:(n + 1) * P],
                                             negd[:, jb:jb + 1].broadcast_to([P, P]), ident[:], start=True, stop=True)
                    m.then_inc(rows_made, 1)
                pe.wait_ge(rows_copied, QUADS)

            def body(t, first):
                def products(k):
                    pe.wait_ge(pT_ready, t * QUADS + k + 1)
                    for n in range(QUAD):
                        m = nc.tensor.matmul(psN[:, 0:F], pT[:, k % 2, n * P:(n + 1) * P], wh[:, k * QUAD + n, :],
                                             start=(k == 0 and n == 0), stop=(k == QUADS - 1 and n == QUAD - 1))
                    m.then_inc(quads_done, 1)

                pe.wait_ge(p_ready, t + 1)
                if not first:
                    pe.wait_ge(neg_ready, t)
                for k in range(QUADS):
                    if k >= 2 or not first:
                        pe.wait_ge(pT_ready, t * QUADS + k - 1)
                    for n in range(QUAD):
                        at = (k * QUAD + n) * P
                        m = nc.tensor.transpose(psP[:, k % 2, n * P:(n + 1) * P], z[:, at:at + P], ident[:])
                    m.then_inc(p_turned, 1)
                    if k >= 1:
                        products(k - 1)
                products(QUADS - 1)

            tiles(pe, body, before)

        @block.scalar
        def _(act):
            def before():
                for k in range(QUADS):
                    act.wait_ge(rows_made, k + 1)
                    nc.scalar.copy(nrow[:, k * QUAD * P:(k + 1) * QUAD * P], psP[:, k % 2]).then_inc(rows_copied, 1)

            def body(t, first):
                act.wait_ge(z_ready, t + 1)
                nc.scalar.activation(z, z, ACT.Exp).then_inc(z_exp, 1)
                for k in range(QUADS):
                    act.wait_ge(p_turned, t * QUADS + k + 1)
                    if k >= 2 or not first:
                        act.wait_ge(quads_done, t * QUADS + k - 1)
                    nc.scalar.copy(pT[:, k % 2], psP[:, k % 2]).then_inc(pT_ready, 1)
                act.wait_ge(neg_ready, t + 1)
                nc.scalar.activation(ex[:], neg[:], ACT.Exp).then_inc(ex_ready, 1)

            tiles(act, body, before)

        @block.vector
        def _(dve):
            STEPS = 14

            def before():
                dve.wait_ge(rows_copied, QUADS)

            def body(t, first):
                done = [0]

                def then(ins):
                    done[0] += 1
                    ins.then_inc(step, 1)
                    dve.wait_ge(step, t * STEPS + done[0])

                ts, tt, stt = nc.vector.tensor_scalar, nc.vector.tensor_tensor, nc.vector.scalar_tensor_tensor
                s = scol[:, bass.ds(t, 1)]
                dve.wait_ge(adjt_in, 16 * (t + 1))
                if not first:
                    dve.wait_ge(quads_done, t * QUADS)
                ts(mask, adjt, 0, None, ALU.is_gt).then_inc(mask_ready, 1)
                dve.wait_ge(mask_ready, t + 1)
                then(ts(z, mask, 1.0, 3e38, ALU.subtract, ALU.mult))
                then(tt(z, z, nrow[:], ALU.subtract))
                then(nc.vector.tensor_reduce(few[:, 0:1], z, AX.X, ALU.max))
                then(ts(few[:, 1:2], few[:, 0:1], s, None, ALU.add))
                then(stt(few[:, 2:3], few[:, 1:2], 0.2, few[:, 1:2], ALU.mult, ALU.max))
                then(ts(z, nrow[:], -1.0, s, ALU.mult, ALU.add))
                then(stt(z, z, 0.2, z, ALU.mult, ALU.max))
                ts(z, z, few[:, 2:3], 0.0, ALU.subtract, ALU.min).then_inc(z_ready, 1)
                dve.wait_ge(z_exp, t + 1)
                tt(z, z, mask, ALU.mult).then_inc(p_ready, 1)
                dve.wait_ge(p_ready, t + 1)
                then(nc.vector.tensor_reduce(few[:, 3:4], z, AX.X, ALU.add))
                then(ts(few[:, 4:5], few[:, 3:4], 0.0, None, ALU.is_equal))
                then(stt(few[:, 5:6], few[:, 4:5], float(N), few[:, 3:4], ALU.mult, ALU.add))
                nc.vector.reciprocal(few[:, 6:7], few[:, 5:6])
                dve.wait_ge(quads_done, (t + 1) * QUADS)
                then(stt(v[:], csum[:], few[:, 4:5], psN[:, 0:F], ALU.mult, ALU.add))
                then(ts(v[:], v[:], few[:, 6:7], None, ALU.mult))
                ts(neg[:], v[:], 0.0, None, ALU.min).then_inc(neg_ready, 1)
                then(ts(v[:], v[:], 0.0, -1.0, ALU.max, ALU.add))
                dve.wait_ge(ex_ready, t + 1)
                dve.wait_ge(xt_in, 16 * (t + 1))
                then(tt(ex[:], ex[:], v[:], ALU.add))
                tt(xt[:], ex[:], xt[:], ALU.add).then_inc(out_ready, 1)
                assert done[0] == STEPS

            tiles(dve, body, before)
    return sems


_INS = ["x", "adj", "L0_gnn_W", "L0_gnn_a", "L1_gnn_W", "L1_gnn_a"]


def kernel(**inputs):
    import numpy as _np
    import concourse.bacc as _bacc
    from concourse import mybir as _mybir
    from concourse.bass_utils import run_bass_kernel_spmd as _run

    nc = _bacc.Bacc("TRN2", target_bir_lowering=False, num_devices=1)
    arrays, args = {}, []
    for name in _INS:
        arr = _np.ascontiguousarray(inputs[name])
        arrays[f"in_{name}_dram"] = arr
        args.append(nc.dram_tensor(f"in_{name}_dram", arr.shape, _mybir.dt.from_np(arr.dtype),
                                   kind="ExternalInput").ap())
    out = nc.dram_tensor("out_0_dram", inputs["x"].shape, _mybir.dt.float32, kind="ExternalOutput").ap()
    build(nc, *args, out)
    r = _run(nc, [arrays], core_ids=[0])
    return r.results[0]["out_0_dram"]
```
